# Optimizing a Trainium2 kernel written in Bass

```python
import numpy as np
import jax
import jax.numpy as jnp

def _softmax(x, axis=-1):
    return jax.nn.softmax(x, axis=axis)

def _gelu(x):
    return jax.nn.gelu(x, approximate=True)

def _silu(x):
    return jax.nn.silu(x)

def _sigmoid(x):
    return jax.nn.sigmoid(x)

def _layernorm(x, axis=-1, eps=1e-05):
    m = jnp.mean(x, axis=axis, keepdims=True)
    v = jnp.var(x, axis=axis, keepdims=True)
    return (x - m) / jnp.sqrt(v + eps)

def _scatter_add(tgt, idx, src, axis=0):
    return tgt.at[idx].add(src)

def _segment_sum(src, seg, n):
    return jax.ops.segment_sum(src, seg, n)
kernel_name = 'mk_xattn_ffn_d2_seqx_r8_916309'

def setup_inputs(seed: int=0):
    np.random.seed(seed)
    _w = jnp.asarray

    def _rec_inputs():
        import jax
        import jax.numpy as jnp
        _rk = jax.random.key(seed)
        x = -0.0002928 + 1 * jax.random.normal(jax.random.fold_in(_rk, 1), (32, 64, 128), jnp.float32)
        _lenS = 64 - jax.random.randint(jax.random.fold_in(_rk, 7), (32,), 0, max(1, 64 // 4) + 1, jnp.int32)
        _lenS2 = 64 - jax.random.randint(jax.random.fold_in(_rk, 8), (32,), 0, max(1, 64 // 4) + 1, jnp.int32)
        _ctx_1024P = jax.random.normal(jax.random.fold_in(_rk, 11), (32, 16, 128), jnp.float32)
        _ctx_1024c = jax.random.dirichlet(jax.random.fold_in(_rk, 511), 0.3 * jnp.ones((16,), jnp.float32), (32, 64))
        _ctx_1024t = jnp.einsum('bsk,bkd->bsd', _ctx_1024c, _ctx_1024P)
        _ctx_1024t = _ctx_1024t * jax.lax.rsqrt(jnp.mean(jnp.square(_ctx_1024t)) + 1e-12) * 0.953939
        ctx_1024 = -1.39393e-06 + 0.999914 * (_ctx_1024t + 0.3 * jax.random.normal(jax.random.fold_in(_rk, 611), (32, 64, 128), jnp.float32))
        return (x, ctx_1024)
    x, ctx_1024 = _rec_inputs()

    def _L0_xattn_setup():
        import jax, jax.numpy as jnp
        import numpy as np
        EMBED_DIM = 128
        NUM_HEADS = 16
        HEAD_DIM = EMBED_DIM // NUM_HEADS
        WINDOW = 128
        key = jax.random.key(seed)
        ks = jax.random.split(key, 11)
        B, S, E = (2, 256, EMBED_DIM)
        scale = 1.0 / np.sqrt(E)
        inp = {'q': jax.random.normal(ks[0], (B, S, E), jnp.float32), 'k': jax.random.normal(ks[1], (B, S, E), jnp.float32), 'v': jax.random.normal(ks[2], (B, S, E), jnp.float32), 'Wq': jax.random.normal(ks[3], (E, E), jnp.float32) * scale, 'bq': jnp.zeros((E,), jnp.float32), 'Wk': jax.random.normal(ks[4], (E, E), jnp.float32) * scale, 'bk': jnp.zeros((E,), jnp.float32), 'Wv': jax.random.normal(ks[5], (E, E), jnp.float32) * scale, 'bv': jnp.zeros((E,), jnp.float32), 'Wo': jax.random.normal(ks[6], (E, E), jnp.float32) * scale, 'bo': jnp.zeros((E,), jnp.float32)}
        return inp
    _L0_xattn_all = _L0_xattn_setup()
    _L0_xattn_in = {k: v for k, v in _L0_xattn_all.items() if k in ('Wq', 'bq', 'Wk', 'bk', 'Wv', 'bv', 'Wo', 'bo')}
    del _L0_xattn_all

    def _L0_ffn_setup():
        import jax, jax.numpy as jnp
        import numpy as np
        B, S, D, M, E, K = (2, 256, 128, 176, 8, 2)
        key = jax.random.key(seed)
        k0, k1, k2, k3, k4 = jax.random.split(key, 5)
        scale = 0.02
        return {'x': jax.random.normal(k0, (B, S, D), dtype=jnp.float32), 'w_gate': jax.random.normal(k1, (D, E), dtype=jnp.float32) * scale, 'w_g': jax.random.normal(k2, (E, D, M), dtype=jnp.float32) * scale, 'w_u': jax.random.normal(k3, (E, D, M), dtype=jnp.float32) * scale, 'w_d': jax.random.normal(k4, (E, M, D), dtype=jnp.float32) * scale}
    _L0_ffn_all = _L0_ffn_setup()
    _L0_ffn_in = {k: v for k, v in _L0_ffn_all.items() if k in ('w_gate', 'w_g', 'w_u', 'w_d')}
    del _L0_ffn_all

    def _L1_xattn_setup():
        import jax, jax.numpy as jnp
        import numpy as np
        DIM = 128
        NUM_HEADS = 16
        HEAD_DIM = DIM // NUM_HEADS
        key = jax.random.key(seed)
        ks = jax.random.split(key, 11)
        B, N, C = (2, 256, DIM)
        s = 1.0 / np.sqrt(C)
        inp = {'q': jax.random.normal(ks[0], (B, N, C), jnp.float32), 'k': jax.random.normal(ks[1], (B, N, C), jnp.float32), 'v': jax.random.normal(ks[2], (B, N, C), jnp.float32), 'Wq': jax.random.normal(ks[3], (C, C), jnp.float32) * s, 'bq': jnp.zeros((C,), jnp.float32), 'Wk': jax.random.normal(ks[4], (C, C), jnp.float32) * s, 'bk': jnp.zeros((C,), jnp.float32), 'Wv': jax.random.normal(ks[5], (C, C), jnp.float32) * s, 'bv': jnp.zeros((C,), jnp.float32), 'Wo': jax.random.normal(ks[6], (C, C), jnp.float32) * s, 'bo': jnp.zeros((C,), jnp.float32)}
        return inp
    _L1_xattn_all = _L1_xattn_setup()
    _L1_xattn_in = {k: v for k, v in _L1_xattn_all.items() if k in ('Wq', 'bq', 'Wk', 'bk', 'Wv', 'bv', 'Wo', 'bo')}
    del _L1_xattn_all

    def _L1_ffn_setup():
        import jax, jax.numpy as jnp
        import numpy as np
        D_MODEL, D_FF, N_EXPERTS, TOP_K = (128, 512, 8, 2)
        key = jax.random.key(seed)
        k0, k1, k2, k3 = jax.random.split(key, 4)
        x = jax.random.normal(k0, (2, 256, D_MODEL), dtype=jnp.float32)
        gate_w = jax.random.normal(k1, (D_MODEL, N_EXPERTS), dtype=jnp.float32) * 0.02
        W1 = jax.random.normal(k2, (N_EXPERTS, D_MODEL, D_FF), dtype=jnp.float32) * 0.02
        b1 = jnp.zeros((N_EXPERTS, D_FF), dtype=jnp.float32)
        W2 = jax.random.normal(k3, (N_EXPERTS, D_FF, D_MODEL), dtype=jnp.float32) * 0.02
        b2 = jnp.zeros((N_EXPERTS, D_MODEL), dtype=jnp.float32)
        return {'x': x, 'gate_w': gate_w, 'W1': W1, 'b1': b1, 'W2': W2, 'b2': b2}
    _L1_ffn_all = _L1_ffn_setup()
    _L1_ffn_in = {k: v for k, v in _L1_ffn_all.items() if k in ('gate_w', 'W1', 'b1', 'W2', 'b2')}
    del _L1_ffn_all
    return {'x': x, 'ctx_1024': ctx_1024, 'L0_xattn_Wq': _L0_xattn_in['Wq'], 'L0_xattn_bq': _L0_xattn_in['bq'], 'L0_xattn_Wk': _L0_xattn_in['Wk'], 'L0_xattn_bk': _L0_xattn_in['bk'], 'L0_xattn_Wv': _L0_xattn_in['Wv'], 'L0_xattn_bv': _L0_xattn_in['bv'], 'L0_xattn_Wo': _L0_xattn_in['Wo'], 'L0_xattn_bo': _L0_xattn_in['bo'], 'L0_ffn_w_gate': _L0_ffn_in['w_gate'], 'L0_ffn_w_g': _L0_ffn_in['w_g'], 'L0_ffn_w_u': _L0_ffn_in['w_u'], 'L0_ffn_w_d': _L0_ffn_in['w_d'], 'L1_xattn_Wq': _L1_xattn_in['Wq'], 'L1_xattn_bq': _L1_xattn_in['bq'], 'L1_xattn_Wk': _L1_xattn_in['Wk'], 'L1_xattn_bk': _L1_xattn_in['bk'], 'L1_xattn_Wv': _L1_xattn_in['Wv'], 'L1_xattn_bv': _L1_xattn_in['bv'], 'L1_xattn_Wo': _L1_xattn_in['Wo'], 'L1_xattn_bo': _L1_xattn_in['bo'], 'L1_ffn_gate_w': _L1_ffn_in['gate_w'], 'L1_ffn_W1': _L1_ffn_in['W1'], 'L1_ffn_b1': _L1_ffn_in['b1'], 'L1_ffn_W2': _L1_ffn_in['W2'], 'L1_ffn_b2': _L1_ffn_in['b2']}

def reference(x, ctx_1024, L0_xattn_Wq, L0_xattn_bq, L0_xattn_Wk, L0_xattn_bk, L0_xattn_Wv, L0_xattn_bv, L0_xattn_Wo, L0_xattn_bo, L0_ffn_w_gate, L0_ffn_w_g, L0_ffn_w_u, L0_ffn_w_d, L1_xattn_Wq, L1_xattn_bq, L1_xattn_Wk, L1_xattn_bk, L1_xattn_Wv, L1_xattn_bv, L1_xattn_Wo, L1_xattn_bo, L1_ffn_gate_w, L1_ffn_W1, L1_ffn_b1, L1_ffn_W2, L1_ffn_b2):
    import jax
    import jax.numpy as jnp

    def _L0_xattn_ref(q, k, v, Wq, bq, Wk, bk, Wv, bv, Wo, bo):
        import jax, jax.numpy as jnp
        import numpy as np
        EMBED_DIM = 128
        NUM_HEADS = 16
        HEAD_DIM = EMBED_DIM // NUM_HEADS
        WINDOW = 128
        B, S, E = q.shape
        H, D = (NUM_HEADS, HEAD_DIM)
        Q = (q @ Wq.T + bq).reshape(B, S, H, D).transpose(0, 2, 1, 3)
        K = (k @ Wk.T + bk).reshape(B, S, H, D).transpose(0, 2, 1, 3)
        V = (v @ Wv.T + bv).reshape(B, S, H, D).transpose(0, 2, 1, 3)
        scores = jnp.einsum('bhqd,bhkd->bhqk', Q, K) / jnp.sqrt(jnp.float32(D))
        idx = jnp.arange(S)
        band = jnp.abs(idx[:, None] - idx[None, :]) <= WINDOW
        scores = jnp.where(band[None, None], scores, -jnp.inf)
        probs = jax.nn.softmax(scores, axis=-1)
        out = jnp.einsum('bhqk,bhkd->bhqd', probs, V)
        out = out.transpose(0, 2, 1, 3).reshape(B, S, E)
        return out @ Wo.T + bo

    def _L0_ffn_ref(x, w_gate, w_g, w_u, w_d):
        import jax, jax.numpy as jnp
        import numpy as np
        B, S, D, M, E, K = (2, 256, 128, 176, 8, 2)
        scores = x @ w_gate
        topk_scores, topk_idx = jax.lax.top_k(scores, K)
        topk_probs = jax.nn.softmax(topk_scores, axis=-1)
        gating = jnp.sum(jax.nn.one_hot(topk_idx, E, dtype=topk_probs.dtype) * topk_probs[..., None], axis=-2)
        hidden = jax.nn.silu(jnp.einsum('bsd,edm->ebsm', x, w_g)) * jnp.einsum('bsd,edm->ebsm', x, w_u)
        expert_out = jnp.einsum('ebsm,emd->ebsd', hidden, w_d)
        y = jnp.einsum('bse,ebsd->bsd', gating, expert_out)
        return y

    def _L1_xattn_ref(q, k, v, Wq, bq, Wk, bk, Wv, bv, Wo, bo):
        import jax, jax.numpy as jnp
        import numpy as np
        DIM = 128
        NUM_HEADS = 16
        HEAD_DIM = DIM // NUM_HEADS
        B, Nq, C = q.shape
        Nkv = k.shape[1]
        H, D = (NUM_HEADS, HEAD_DIM)
        qh = (q @ Wq.T + bq).reshape(B, Nq, H, D).transpose(0, 2, 1, 3)
        kh = (k @ Wk.T + bk).reshape(B, Nkv, H, D).transpose(0, 2, 1, 3)
        vh = (v @ Wv.T + bv).reshape(B, Nkv, H, D).transpose(0, 2, 1, 3)
        scale = D ** (-0.5)
        attn = jax.nn.softmax(jnp.einsum('bhqd,bhkd->bhqk', qh, kh) * scale, axis=-1)
        out = jnp.einsum('bhqk,bhkd->bhqd', attn, vh)
        out = out.transpose(0, 2, 1, 3).reshape(B, Nq, C)
        return out @ Wo.T + bo

    def _L1_ffn_ref(x, gate_w, W1, b1, W2, b2):
        import jax, jax.numpy as jnp
        import numpy as np
        D_MODEL, D_FF, N_EXPERTS, TOP_K = (128, 512, 8, 2)
        orig_shape = x.shape
        xf = x.reshape(-1, D_MODEL)
        n_tokens = xf.shape[0]
        router_logits = xf @ gate_w
        topk_vals, topk_idx = jax.lax.top_k(router_logits, TOP_K)
        topk_w = jax.nn.softmax(topk_vals, axis=-1)
        comb = jnp.zeros((n_tokens, N_EXPERTS), dtype=x.dtype)
        comb = comb.at[jnp.arange(n_tokens)[:, None], topk_idx].add(topk_w)
        h = jax.nn.gelu(jnp.einsum('nd,edf->enf', xf, W1) + b1[:, None, :], approximate=False)
        y = jnp.einsum('enf,efd->end', h, W2) + b2[:, None, :]
        out = jnp.einsum('ne,end->nd', comb, y)
        return out.reshape(orig_shape)
    x = x + _L0_xattn_ref(_layernorm(x, axis=-1), ctx_1024, ctx_1024, L0_xattn_Wq, L0_xattn_bq, L0_xattn_Wk, L0_xattn_bk, L0_xattn_Wv, L0_xattn_bv, L0_xattn_Wo, L0_xattn_bo)
    x = x + _L0_ffn_ref(_layernorm(x, axis=-1), L0_ffn_w_gate, L0_ffn_w_g, L0_ffn_w_u, L0_ffn_w_d)
    x = x + _L1_xattn_ref(_layernorm(x, axis=-1), ctx_1024, ctx_1024, L1_xattn_Wq, L1_xattn_bq, L1_xattn_Wk, L1_xattn_bk, L1_xattn_Wv, L1_xattn_bv, L1_xattn_Wo, L1_xattn_bo)
    x = x + _L1_ffn_ref(_layernorm(x, axis=-1), L1_ffn_gate_w, L1_ffn_W1, L1_ffn_b1, L1_ffn_W2, L1_ffn_b2)
    return x

_drawn_inputs = setup_inputs


def setup_inputs(seed=0):
    import zlib

    import numpy as np

    out = dict(_drawn_inputs(seed))
    spreads = {'L0_xattn_bq': (0.0, 0.404),
     'L0_xattn_bk': (0.0, 2.0),
     'L0_xattn_bv': (0.0, 0.1),
     'L0_xattn_bo': (0.0, 0.1),
     'L1_xattn_bq': (0.0, 1.211),
     'L1_xattn_bk': (0.0, 2.0),
     'L1_xattn_bv': (0.0, 0.372),
     'L1_xattn_bo': (0.0, 0.303),
     'L1_ffn_b1': (0.0, 0.696),
     'L1_ffn_b2': (0.0, 0.424)}
    factors = {'L0_ffn_w_gate': 8.0,
     'L0_ffn_w_g': 8.0,
     'L0_ffn_w_u': 8.0,
     'L0_ffn_w_d': 8.0,
     'L1_ffn_W1': 4.701}
    for name, (base, spread) in spreads.items():
        noise = np.random.default_rng([zlib.crc32(name.encode()), seed]).standard_normal(out[name].shape)
        drawn = base * np.exp(spread * noise) if base else spread * noise
        out[name] = jnp.asarray(drawn.astype(out[name].dtype))
    for name, factor in factors.items():
        out[name] = (out[name] * factor).astype(out[name].dtype)
    return out
```

```python
from contextlib import ExitStack

import numpy as np

import concourse.bass as bass
from concourse import mybir

F32 = mybir.dt.float32
F16 = mybir.dt.float16
U32 = mybir.dt.uint32
ALU = mybir.AluOpType
ACT = mybir.ActivationFunctionType
AX = mybir.AxisListType

P = 128
SEQ = 64
PER_TILE = P // SEQ
D = 128
HEADS = 16
HD = D // HEADS
PAIRS = HEADS // 2
VW = HD + 1
EXPERTS = 8
M0 = 176
M1 = 512
HID0 = EXPERTS * M0
STEPS0 = HID0 // P
STEPS1 = M1 // P
G = 4
EPS = 1e-5
WSCALE = 1024.0
HI_ROW, LO_ROW, HI2_ROW = 0, 32, 64


def positive_wait(eng, sem, value):
    if not isinstance(value, int) or value > 0:
        eng.wait_ge(sem, value)


def pipeline(eng, step, tiles, behind, ahead):
    first = 2 - behind
    last = (tiles - ahead - first) // 2 * 2 + first
    for t in range(-ahead, first):
        step(t, 0)
    with eng.Fori(0, (last - first) // 2) as i:
        step(2 * i + first, 0)
        step(2 * i + (first + 1), 1)
    for t in range(last, tiles):
        step(t, 0)


def build(nc, a, out):
    tokens = a["x"].shape[0] * a["x"].shape[1]
    TILES = tokens // P
    GROUPS = TILES // G
    GT = G * P

    with ExitStack() as ctx:
        def sb(name, shape, dt):
            return ctx.enter_context(nc.sbuf_tensor(name, shape, dt))

        def sems(names, suffix=""):
            return {n: ctx.enter_context(nc.semaphore(n + suffix)) for n in names.split()}

        x = sb("x_res", [P, TILES, D], F32)
        mv = sb("mean_var", [P, TILES, 2], F32)
        rstd = sb("rstd", [P, TILES], F32)
        mv_now = sb("mv_now", [P, 2, 2], F32)
        zero_eps = sb("zero_eps", [P, 2], F32)
        wait_carrier = sb("wait_carrier", [P, 2], F32)
        b1_now = sb("b1_now", [P, STEPS1], F32)
        minus_half = sb("minus_half", [P, 1], F32)
        stats = sb("stats", [P, 2, 6], F32)
        ident = sb("ident", [P, P], F32)
        ident16 = sb("ident16", [P, P], F16)
        iota8 = sb("iota8", [P, EXPERTS], F32)
        expert_rows = sb("expert_rows", [P, HID0], F16)
        two_rows = sb("two_rows", [P, P], F16)
        w_raw = sb("w_raw", [P, 8, P], F32)
        wT = sb("wT", [P, 2, 8, P], F16)
        col_raw = sb("col_raw", [P, P], F32)
        cols = sb("cols", [P, P], F32)
        N_B1 = EXPERTS * STEPS1
        bias_col = cols[:, N_B1:N_B1 + 4]
        b1_col = cols[:, 0:N_B1].rearrange("p (e j) -> p e j", j=STEPS1)
        bias_raw = sb("bias_raw", [33, 4, P], F32)
        bias_hi = sb("bias_hi", [33, 4, P], F16)
        bias_rows = sb("bias_rows", [P, 4, P], F16)
        gate_raw = sb("gate_raw", [P, 2, EXPERTS], F32)
        gate_w = sb("gate_w", [P, 2, 2, EXPERTS], F16)
        b2_raw = sb("b2_raw", [P, D], F32)
        b2_hi = sb("b2_hi", [P, D], F16)
        b2_rows = sb("b2_rows", [P, D], F16)
        ctx_T = sb("ctx_T", [P, 2, tokens], F16)
        kT = [sb(f"kT{l}", [P, TILES, 2, PER_TILE, SEQ], F16) for l in range(2)]
        vals = sb("vals", [P, TILES, 2, PAIRS, PER_TILE, 2, VW], F16)
        k_blocks = sb("k_blocks", [P, 2, 2, PER_TILE, HEADS * SEQ], F16)
        wg = sb("wg", [P, 2, HID0], F16)
        wu = sb("wu", [P, 2, HID0], F16)
        wd = sb("wd", [P, 2, HID0], F16)
        w1 = sb("w1", [P, 2, EXPERTS, M1], F16)
        w2 = sb("w2", [P, 2, EXPERTS, STEPS1, D], F16)
        w_stage = sb("w_stage", [P, 2, HID0], F32)
        area = sb("area", [P, 12800], F32)
        used = [0]

        def carve(shape, dt):
            n = int(np.prod(shape)) * (2 if dt == F16 else 4) // 4
            ap = area[:, used[0]:used[0] + n]
            used[0] += n
            assert used[0] <= 12800, used
            if dt == F16:
                ap = ap.bitcast(F16)
            names = "abcd"[:len(shape)]
            if len(shape) > 1:
                ap = ap.rearrange(f"p ({' '.join(names)}) -> p {' '.join(names)}", **dict(zip(names[1:], shape[1:])))
            return ap

        xhat = carve([2, P], F32)
        xT = carve([2, 2, P], F16)
        q_f = carve([2, P], F32)
        q_hl = carve([2, 2, P], F16)
        mx = carve([2, HEADS], F32)
        probs = carve([2, HEADS * SEQ], F32)
        pT = carve([2, 2, PAIRS, P], F16)
        rden = carve([2, HEADS], F32)
        o_n = carve([2, P], F32)
        oT = carve([2, 2, P], F16)
        used[0] = 0
        ctx_raw = carve([TILES, D], F32)
        k_f = carve([2, GT], F32)
        v_f = carve([2, GT], F32)
        used[0] = 0
        fx = carve([2, G * P], F32)
        xTa = carve([2, tokens], F16)
        logits = carve([TILES, EXPERTS], F32)
        top_v = carve([TILES, 8], F32)
        top_i = carve([TILES, 8], F32).bitcast(U32)
        top_f = carve([TILES, 2], F32)
        diff = carve([TILES], F32)
        prob = carve([TILES, 2], F32)
        one_hot = carve([2, TILES, EXPERTS], F32)
        comb = carve([TILES, EXPERTS], F32)
        comb16 = carve([TILES, P], F16)
        combT = carve([tokens], F16)
        act_f = carve([2, GT], F32)
        gated = carve([2, GT], F32)
        hid = carve([2, 2, GT], F16)

        ps = ctx.enter_context(nc.psum_tensor("ps", [P, 8, 512], F32))
        half_bank = [ps[:, b, :].bitcast(F16) for b in range(8)]

        s = sems("ld_x0 ld_x1 ld_x2 ld_x3 ld_c ld_w ld_k ld_s col_ps cols ids ones cast16 wt_ps wt_hi wt_lo ct_ps ct_hi ct_lo bias_h bias_l "
                 "b2h b2l gate_h gate_l zero vone mh st agg ag rs out_d "
                 "chunk0 chunk1 ch_hi ch_f ch_lo cst")
        KV = [sems("k_ps k_f k_hi k_lo v_ps v_f v_w", f"_kv{l}") for l in range(2)]
        A = [sems("kb0 kb1 xh xt_ps xt_hi xt_lo q_ps q_act q_lo s_ps mx sub ex p_ps p_hi p_lo o_ps rd on "
                  "ot_ps ot_hi ot_lo y_ps res", f"_a{l}") for l in range(2)]
        F = [sems("xh xt_ps xt_hi xt_lo lg_ps lg top idx dif ex pr oh cb c16 ct_ps ct_hi ct_lo "
                  "b1 up act t1 gt hi lo down res b2_ps b2_r", f"_f{l}") for l in range(2)]

        CHUNKS0 = 3
        w_in = [a["L0_ffn_w_g"].rearrange("e d m -> d e m"), a["L0_ffn_w_u"].rearrange("e d m -> d e m"),
                a["L0_ffn_w_d"].rearrange("e m d -> (e m) d").rearrange("(j p) d -> p j d", p=P)]
        w_out = [wg, wu, wd]
        chunks = [(src, "e", w[:, 0, :], w[:, 1, :]) for src, w in zip(w_in, w_out)]
        for e in range(0, EXPERTS, 2):
            chunks.append((a["L1_ffn_W1"][e:e + 2].rearrange("e d f -> d e f"), "w1",
                           w1[:, 0, e:e + 2, :].rearrange("p e f -> p (e f)"), w1[:, 1, e:e + 2, :].rearrange("p e f -> p (e f)")))
        for e in range(0, EXPERTS, 2):
            chunks.append((a["L1_ffn_W2"][e:e + 2].rearrange("e (j p) d -> p (e j) d", p=P), "w2",
                           w2[:, 0, e:e + 2].rearrange("p e j d -> p (e j d)"), w2[:, 1, e:e + 2].rearrange("p e j d -> p (e j d)")))
        x_dram = a["x"].rearrange("b s d -> (b s) d").rearrange("(t p) d -> p t d", p=P)
        c_dram = a["ctx_1024"].rearrange("b s d -> (b s) d").rearrange("(t p) d -> p t d", p=P)
        out_dram = out.rearrange("b s d -> (b s) d").rearrange("(t p) d -> p t d", p=P)
        W_NAMES = [f"L{l}_xattn_W{n}" for l in range(2) for n in "qkvo"]

        def alive(t):
            return not isinstance(t, int) or 0 <= t < TILES

        block = ctx.enter_context(nc.Block())

        @block.sync
        def _(sp):
            sp.dma_start(ident[:, :], a["ident"]).then_inc(s["ids"], 16)
            for n, name in enumerate(W_NAMES):
                sp.dma_start(w_raw[:, n, :], a[name]).then_inc(s["ld_w"], 16)
            for g in range(GROUPS):
                sp.dma_start(ctx_raw[:, G * g:G * (g + 1), :], c_dram[:, G * g:G * (g + 1), :]).then_inc(s["ld_c"], 16)
            sp.dma_start(iota8[:, :], a["iota8"]).then_inc(s["cst"], 16)
            sp.dma_start(expert_rows[:, :], a["expert_rows"]).then_inc(s["cst"], 16)
            sp.dma_start(two_rows[:, :], a["two_rows"]).then_inc(s["cst"], 16)

            def key_blocks(l):
                q = A[l]
                sp.wait_ge(KV[l]["k_hi"], GROUPS)
                sp.wait_ge(KV[l]["k_lo"], GROUPS)
                if l == 0:
                    sp.wait_ge(s["zero"], 1)
                else:
                    sp.wait_ge(A[0]["s_ps"], TILES)

                def tile(t, par):
                    sem = (q["kb0"], q["kb1"])[par]
                    for h in range(HEADS):
                        r = slice(h * HD, (h + 1) * HD)
                        dst = k_blocks[r, par, :, :, h * SEQ:(h + 1) * SEQ].rearrange("p a b k -> p (a b) k")
                        src = kT[l][r, t, :, :, :].rearrange("p a b k -> p (a b) k")
                        sp.dma_start(dst, src).then_inc(sem, 16)

                tile(0, 0)
                tile(1, 1)
                with sp.Fori(1, TILES // 2) as i:
                    for u in range(2):
                        sp.wait_ge(q["s_ps"], 2 * i + (u - 1))
                        tile(2 * i + u, u)

            key_blocks(0)
            key_blocks(1)
            for g in range(GROUPS):
                sp.wait_ge(F[1]["res"], (EXPERTS - 1) * GROUPS + g + 1)
                sp.dma_start(out_dram[:, G * g:G * (g + 1), :], x[:, G * g:G * (g + 1), :]).then_inc(s["out_d"], 16)
            sp.wait_ge(s["out_d"], 16 * GROUPS)

        @block.scalar
        def _(act):
            act.wait_ge(s["ones"], 1)
            for g in range(GROUPS):
                act.dma_start(x[:, G * g:G * (g + 1), :], x_dram[:, G * g:G * (g + 1), :]).then_inc((s["ld_x0"], s["ld_x1"], s["ld_x2"], s["ld_x3"])[g], 16)
            for n, name in enumerate(["L0_xattn_bq", "L0_xattn_bk", "L1_xattn_bq", "L1_xattn_bk"]):
                act.dma_start(col_raw[N_B1 + n:N_B1 + n + 1, :], a[name].rearrange("(o p) -> o p", o=1)).then_inc(s["ld_k"], 16)
            act.dma_start(col_raw[0:N_B1, :], a["L1_ffn_b1"].rearrange("e (j p) -> (e j) p", p=P)).then_inc(s["ld_k"], 16)
            for n, name in enumerate(["L0_xattn_bv", "L0_xattn_bo", "L1_xattn_bv", "L1_xattn_bo"]):
                for r in (0, 32):
                    act.dma_start(bias_raw[r:r + 1, n, :], a[name].rearrange("(o p) -> o p", o=1)).then_inc(s["ld_s"], 16)
            act.dma_start(gate_raw[:, 0, :], a["L0_ffn_w_gate"]).then_inc(s["ld_s"], 16)
            act.dma_start(gate_raw[:, 1, :], a["L1_ffn_gate_w"]).then_inc(s["ld_s"], 16)
            for r in (HI_ROW, LO_ROW, HI2_ROW):
                act.dma_start(b2_raw[r:r + EXPERTS, :], a["L1_ffn_b2"]).then_inc(s["ld_s"], 16)

            act.wait_ge(s["col_ps"], 1)
            nc.scalar.activation(cols[:, :], ps[:, 6, 0:P], ACT.Copy).then_inc(s["cols"], 1)
            for h in range(2):
                act.wait_ge(s["wt_ps"], h + 1)
                nc.scalar.activation(wT[:, 0, 4 * h:4 * h + 4, :], ps[:, h, :].rearrange("p (a b) -> p a b", a=4),
                                     ACT.Copy, scale=WSCALE).then_inc(s["wt_hi"], 1)
            for g in range(GROUPS):
                act.wait_ge(s["ct_ps"], g + 1)
                nc.scalar.activation(ctx_T[:, 0, g * GT:(g + 1) * GT], ps[:, 2 + g, :], ACT.Copy).then_inc(s["ct_hi"], 1)

            def keys_values(l):
                q = KV[l]
                act.wait_ge(s["cols"], 1)
                for g in range(GROUPS):
                    act.wait_ge(q["k_ps"], g + 1)
                    if g >= 2:
                        act.wait_ge(q["k_lo"], g - 1)
                    nc.scalar.activation(k_f[:, g % 2, :], ps[:, g % 2, :], ACT.Identity,
                                         bias=bias_col[:, 2 * l + 1:2 * l + 2], scale=1 / WSCALE).then_inc(q["k_f"], 1)
                for j in range(TILES // 2):
                    act.wait_ge(q["v_ps"], j + 1)
                    if j >= 2:
                        act.wait_ge(q["v_w"], 4 * (j - 1))
                    nc.scalar.activation(v_f[:, j % 2, :], ps[:, 4 + j % 2, :], ACT.Copy,
                                         scale=1 / WSCALE).then_inc(q["v_f"], 1)

            def attention(l):
                q = A[l]

                def step(t, u):
                    par = lambda k: (u + k) % 2 if not isinstance(t, int) else (t + k) % 2
                    if alive(t):
                        act.wait_ge(q["ot_ps"], t + 1)
                        positive_wait(act, q["y_ps"], t - 1)
                        nc.scalar.activation(oT[:, par(0), 0, :], ps[:, 6, 0:P], ACT.Copy).then_inc(q["ot_hi"], 1)
                    if alive(t + 3):
                        act.wait_ge(q["xt_ps"], t + 4)
                        positive_wait(act, q["q_ps"], t + 2)
                        nc.scalar.activation(xT[:, par(3), 0, :], ps[:, 4, 0:P], ACT.Copy).then_inc(q["xt_hi"], 1)
                    if alive(t + 1):
                        positive_wait(act, q["o_ps"], t)
                        for h in range(2):
                            act.wait_ge(q["p_ps"], 2 * t + (3 + h))
                            nc.scalar.activation(pT[:, par(1), 0, 4 * h:4 * h + 4, :],
                                                 ps[:, 2 + h, :].rearrange("p (a b) -> p a b", a=4),
                                                 ACT.Copy).then_inc(q["p_hi"], 1)
                    if alive(t + 3):
                        act.wait_ge(q["q_ps"], t + 4)
                        positive_wait(act, q["q_lo"], t + 2)
                        positive_wait(act, q["s_ps"], t + 2)
                        for o in (q_f[:, par(3), :], q_hl[:, par(3), 0, :]):
                            nc.scalar.activation(o, ps[:, 4, P:2 * P], ACT.Identity, bias=bias_col[:, 2 * l:2 * l + 1],
                                                 scale=1 / WSCALE).then_inc(q["q_act"], 1)
                    if alive(t + 2):
                        act.wait_ge(q["sub"], t + 3)
                        nc.scalar.activation(probs[:, par(2), :], probs[:, par(2), :], ACT.Exp,
                                             scale=float(HD) ** -0.5).then_inc(q["ex"], 1)

                pipeline(act, step, TILES, 0, 4)

            def routing(l):
                q = F[l]
                for g in range(GROUPS):
                    act.wait_ge(q["xt_ps"], g + 1)
                    nc.scalar.activation(xTa[:, 0, g * GT:(g + 1) * GT], ps[:, g % 2, :], ACT.Copy).then_inc(q["xt_hi"], 1)
                act.wait_ge(q["dif"], 1)
                nc.scalar.activation(prob[:, :, 1], diff, ACT.Exp).then_inc(q["ex"], 1)
                act.wait_ge(q["ct_ps"], 1)
                nc.scalar.activation(combT[:, 0:tokens // 2], half_bank[2], ACT.Copy).then_inc(q["ct_hi"], 1)

            def experts0():
                q = F[0]
                with act.Fori(0, GROUPS // 2) as i:
                    for k in range(2 * STEPS0 + 1):
                        n = 2 * STEPS0 * i + k
                        if k < 2 * STEPS0:
                            act.wait_ge(q["up"], n + 1)
                            if k >= 2:
                                act.wait_ge(q["t1"], n - 1)
                            nc.scalar.activation(act_f[:, k % 2, :], ps[:, k % 2, :], ACT.Silu,
                                                 scale=1 / WSCALE).then_inc(q["act"], 1)
                        if k >= 1:
                            act.wait_ge(q["gt"], n)
                            if k >= 3:
                                act.wait_ge(q["down"], n - 2)
                            nc.scalar.activation(hid[:, (k - 1) % 2, 0, :], gated[:, (k - 1) % 2, :],
                                                 ACT.Copy).then_inc(q["hi"], 1)

            def experts1():
                q = F[1]
                K = GROUPS * STEPS1
                with act.Fori(0, EXPERTS) as e:
                    nc.scalar.activation(b1_now[:, :], b1_col[:, e, :], ACT.Copy).then_inc(q["b1"], 1)
                    act.wait_ge(q["b1"], e + 1)
                    for k in range(K + 1):
                        n = K * e + k
                        if k < K:
                            act.wait_ge(q["up"], n + 1)
                            if k >= 2:
                                act.wait_ge(q["lo"], n - 1)
                            nc.scalar.activation(act_f[:, k % 2, :], ps[:, k % 4, :], ACT.Gelu,
                                                 bias=b1_now[:, k % STEPS1:k % STEPS1 + 1], scale=1 / WSCALE).then_inc(q["act"], 1)
                        if k >= 1:
                            act.wait_ge(q["act"], n)
                            if k >= 3:
                                act.wait_ge(q["down"], n - 2)
                            nc.scalar.activation(hid[:, (k - 1) % 2, 0, :], act_f[:, (k - 1) % 2, :],
                                                 ACT.Copy).then_inc(q["hi"], 1)

            keys_values(0)
            attention(0)
            routing(0)
            experts0()
            act.wait_ge(F[0]["res"], GROUPS)
            keys_values(1)
            attention(1)
            act.wait_ge(s["ld_s"], 16 * (8 + 2 + 3))
            routing(1)
            experts1()

        @block.gpsimd
        def _(pool):
            nc.gpsimd.memset(minus_half[:, :], -0.5).then_inc(s["mh"], 1)
            nc.gpsimd.memset(k_blocks[:, :, :, :, :], 0.0).then_inc(s["zero"], 1)

            def rstds(l):
                with pool.Fori(0, TILES) as t:
                    pool.wait_ge(s["ag"], t + (TILES * l + 1))
                    nc.gpsimd.tensor_tensor(rstd[:, bass.ds(t, 1)], mv[:, t, 1:2], minus_half[:, :], ALU.pow).then_inc(s["rs"], 1)

            pool.wait_ge(s["mh"], 1)
            rstds(0)
            def load(c):
                src = chunks[c][0]
                n = src.shape[1] * src.shape[2]
                dst = w_stage[:, c % 2, 0:n].rearrange("p (a b) -> p a b", b=src.shape[2])
                pool.dma_start(dst, src).then_inc((s["chunk0"], s["chunk1"])[c % 2], 16)
            load(0)
            load(1)
            for c, (src, _, hi, lo) in enumerate(chunks):
                n = src.shape[1] * src.shape[2]
                raw = w_stage[:, c % 2, 0:n]
                pool.wait_ge((s["chunk0"], s["chunk1"])[c % 2], 16 * (c // 2 + 1))
                nc.gpsimd.tensor_scalar(hi, raw, WSCALE, 1.0, ALU.mult, ALU.mult).then_inc(s["ch_hi"], 1)
                pool.wait_ge(s["ch_hi"], c + 1)
                nc.gpsimd.tensor_scalar(raw, raw, WSCALE, 1.0, ALU.mult, ALU.mult).then_inc(s["ch_f"], 1)
                pool.wait_ge(s["ch_f"], c + 1)
                nc.gpsimd.tensor_tensor(lo, raw, hi, ALU.subtract).then_inc(s["ch_lo"], 1)
                if c + 2 < len(chunks):
                    pool.wait_ge(s["ch_lo"], c + 1)
                    load(c + 2)
            rstds(1)
            q = F[0]
            with pool.Fori(0, GROUPS // 2) as i:
                for k in range(2 * STEPS0):
                    n = 2 * STEPS0 * i + k
                    pool.wait_ge(q["hi"], n + 1)
                    nc.gpsimd.tensor_tensor(hid[:, k % 2, 1, :], gated[:, k % 2, :], hid[:, k % 2, 0, :],
                                            ALU.subtract).then_inc(q["lo"], 1)
            rstds(2)
            rstds(3)

        @block.vector
        def _(dve):
            def carry_wait():
                nc.vector.tensor_copy(wait_carrier[:, 1:2], wait_carrier[:, 0:1])

            def statistics(n, t, par):
                carry_wait()
                nc.vector.bn_stats(stats[:, par, :], x[:, t, :]).then_inc(s["st"], 1)
                dve.wait_ge(s["st"], n + 1)
                carry_wait()
                nc.vector.bn_aggr(mv_now[:, par, :], stats[:, par, :]).then_inc(s["agg"], 1)
                dve.wait_ge(s["agg"], n + 1)
                nc.vector.tensor_tensor(mv[:, t, :], mv_now[:, par, :], zero_eps[:, :], ALU.add).then_inc(s["ag"], 1)

            nc.vector.memset(col_raw[:, :], 0.0).then_inc(s["ones"], 1)
            nc.vector.memset(wait_carrier[:, :], 0.0)
            nc.vector.memset(zero_eps[:, 0:1], 0.0)
            nc.vector.memset(zero_eps[:, 1:2], EPS).then_inc(s["ones"], 1)
            nc.vector.memset(bias_rows[:, :, :], 0.0).then_inc(s["ones"], 1)
            nc.vector.memset(b2_rows[:, :], 0.0).then_inc(s["ones"], 1)
            nc.vector.memset(vals[:, :, :, :, :, :, :], 0.0).then_inc(s["ones"], 1)
            dve.wait_ge(s["ones"], 5)
            for h2 in range(2):
                r = slice(64 * h2, 64 * h2 + 64)
                nc.vector.memset(vals[r, :, 0, :, :, h2, HD:VW].rearrange("p t a b o -> p t (a b) o"), 1.0).then_inc(s["vone"], 1)
            dve.wait_ge(s["ids"], 16)
            nc.vector.tensor_copy(ident16[:, :], ident[:, :]).then_inc(s["cast16"], 1)
            for t in range(TILES):
                dve.wait_ge((s["ld_x0"], s["ld_x1"], s["ld_x2"], s["ld_x3"])[t // G], 16)
                statistics(t, t, t % 2)
            for h in range(2):
                dve.wait_ge(s["wt_hi"], h + 1)
                nc.vector.scalar_tensor_tensor(wT[:, 1, 4 * h:4 * h + 4, :].rearrange("p a b -> p (a b)"), ps[:, h, :], WSCALE,
                                               wT[:, 0, 4 * h:4 * h + 4, :].rearrange("p a b -> p (a b)"),
                                               ALU.mult, ALU.subtract).then_inc(s["wt_lo"], 1)
            for g in range(GROUPS):
                dve.wait_ge(s["ct_hi"], g + 1)
                r = slice(g * GT, (g + 1) * GT)
                nc.vector.tensor_tensor(ctx_T[:, 1, r], ps[:, 2 + g, :], ctx_T[:, 0, r], ALU.subtract).then_inc(s["ct_lo"], 1)
            dve.wait_ge(s["ld_s"], 16 * (8 + 2 + 3))
            nc.vector.tensor_scalar(bias_rows[0:1, :, :], bias_raw[0:1, :, :], WSCALE, None, ALU.mult).then_inc(s["bias_h"], 1)
            nc.vector.tensor_scalar(bias_hi[32:33, :, :], bias_raw[32:33, :, :], WSCALE, None, ALU.mult).then_inc(s["bias_h"], 1)
            for r in (HI_ROW, LO_ROW):
                nc.vector.tensor_scalar(b2_rows[r:r + EXPERTS, :], b2_raw[r:r + EXPERTS, :], WSCALE, None, ALU.mult).then_inc(s["b2h"], 1)
            r = slice(HI2_ROW, HI2_ROW + EXPERTS)
            nc.vector.tensor_scalar(b2_hi[r, :], b2_raw[r, :], WSCALE, None, ALU.mult).then_inc(s["b2h"], 1)
            for l in range(2):
                nc.vector.tensor_scalar(gate_w[:, l, 0, :], gate_raw[:, l, :], WSCALE, None, ALU.mult).then_inc(s["gate_h"], 1)
            dve.wait_ge(s["bias_h"], 2)
            nc.vector.scalar_tensor_tensor(bias_rows[32:33, :, :], bias_raw[32:33, :, :], WSCALE, bias_hi[32:33, :, :],
                                           ALU.mult, ALU.subtract).then_inc(s["bias_l"], 1)
            dve.wait_ge(s["b2h"], 3)
            nc.vector.scalar_tensor_tensor(b2_rows[r, :], b2_raw[r, :], WSCALE, b2_hi[r, :], ALU.mult, ALU.subtract).then_inc(s["b2l"], 1)
            dve.wait_ge(s["gate_h"], 2)
            for l in range(2):
                nc.vector.scalar_tensor_tensor(gate_w[:, l, 1, :], gate_raw[:, l, :], WSCALE, gate_w[:, l, 0, :],
                                               ALU.mult, ALU.subtract).then_inc(s["gate_l"], 1)

            def keys_values(l):
                q = KV[l]
                for g in range(GROUPS):
                    dve.wait_ge(q["k_f"], g + 1)
                    hi, lo = (kT[l][:, G * g:G * (g + 1), c, :, :].rearrange("p t b k -> p t (b k)") for c in range(2))
                    f = k_f[:, g % 2, :].rearrange("p (t k) -> p t k", t=G)
                    nc.vector.tensor_copy(hi, f).then_inc(q["k_hi"], 1)
                    dve.wait_ge(q["k_hi"], g + 1)
                    nc.vector.tensor_tensor(lo, f, hi, ALU.subtract).then_inc(q["k_lo"], 1)
                for j in range(TILES // 2):
                    dve.wait_ge(q["v_f"], j + 1)
                    if l == 1 and j == 0:
                        dve.wait_ge(A[0]["o_ps"], TILES)
                    parts = []
                    for h2 in range(2):
                        rows = slice(64 * h2, 64 * h2 + 64)
                        f = v_f[rows, j % 2, :].rearrange("p (s a h v) -> p s a h v", s=4, h=2, v=HD)
                        for i in range(2):
                            hi, lo = (vals[rows, 2 * j + i, c, :, :, h2, 0:HD].rearrange("p a b v -> p b a v") for c in range(2))
                            parts.append((hi, lo, f[:, 2 * i:2 * i + 2, :, h2, :]))
                    for n, (hi, lo, f) in enumerate(parts):
                        nc.vector.tensor_copy(hi, f).then_inc(s["vone"], 1)
                    dve.wait_ge(s["vone"], 2 + 4 * (j + 1) + 4 * (TILES // 2) * l)
                    for n, (hi, lo, f) in enumerate(parts):
                        nc.vector.tensor_tensor(lo, f, hi, ALU.subtract).then_inc(q["v_w"], 1)

            def attention(l):
                q = A[l]
                inv = 1 / WSCALE

                def step(t, u):
                    par = lambda k: (u + k) % 2 if not isinstance(t, int) else (t + k) % 2
                    if alive(t):
                        dve.wait_ge(q["o_ps"], t + 1)
                        positive_wait(dve, q["ot_ps"], t - 1)
                        for b in range(PER_TILE):
                            rows = slice(64 * b, 64 * b + 64)
                            o = ps[rows, 5, 0:PAIRS * PER_TILE * 2 * VW].rearrange("p (a b h v) -> p a b h v", b=2, h=2, v=VW)
                            nc.vector.reciprocal(rden[rows, par(0), :].rearrange("p (a h) -> p a h", h=2),
                                                 o[:, :, b, :, HD]).then_inc(q["rd"], 1)
                        for b in range(PER_TILE):
                            rows = slice(64 * b, 64 * b + 64)
                            o = ps[rows, 5, 0:PAIRS * PER_TILE * 2 * VW].rearrange("p (a b h v) -> p a b h v", b=2, h=2, v=VW)
                            dve.wait_ge(q["rd"], 2 * t + (1 + b))
                            nc.vector.tensor_tensor(
                                o_n[rows, par(0), :].rearrange("p (a h v) -> p a h v", h=2, v=HD), o[:, :, b, :, 0:HD],
                                rden[rows, par(0), :].rearrange("p (a h o) -> p a h o", h=2, o=1).broadcast_to([64, PAIRS, 2, HD]),
                                ALU.mult).then_inc(q["on"], 1)
                    if alive(t + 2):
                        dve.wait_ge(q["s_ps"], t + 3)
                        positive_wait(dve, q["sub"], t + 1)
                        sc = ps[:, 0:2, :].rearrange("p b (h k) -> p (b h) k", k=SEQ)
                        nc.vector.tensor_reduce(mx[:, par(2), :], sc, axis=AX.X, op=ALU.max).then_inc(q["mx"], 1)
                        dve.wait_ge(q["mx"], t + 3)
                        positive_wait(dve, q["p_ps"], 2 * t + 2)
                        nc.vector.tensor_tensor(
                            probs[:, par(2), :].rearrange("p (h k) -> p h k", k=SEQ), sc,
                            mx[:, par(2), :].unsqueeze(2).broadcast_to([P, HEADS, SEQ]), ALU.subtract).then_inc(q["sub"], 1)
                    if alive(t):
                        dve.wait_ge(q["ot_hi"], t + 1)
                        positive_wait(dve, q["y_ps"], t - 1)
                        nc.vector.tensor_tensor(oT[:, par(0), 1, :], ps[:, 6, 0:P], oT[:, par(0), 0, :],
                                                ALU.subtract).then_inc(q["ot_lo"], 1)
                    if alive(t + 3):
                        dve.wait_ge(q["xt_hi"], t + 4)
                        positive_wait(dve, q["q_ps"], t + 2)
                        nc.vector.tensor_tensor(xT[:, par(3), 1, :], ps[:, 4, 0:P], xT[:, par(3), 0, :],
                                                ALU.subtract).then_inc(q["xt_lo"], 1)
                    if alive(t + 1):
                        positive_wait(dve, q["o_ps"], t)
                        for h in range(2):
                            dve.wait_ge(q["p_hi"], 2 * t + (3 + h))
                            nc.vector.tensor_tensor(pT[:, par(1), 1, 4 * h:4 * h + 4, :].rearrange("p a b -> p (a b)"),
                                                    ps[:, 2 + h, :], pT[:, par(1), 0, 4 * h:4 * h + 4, :].rearrange("p a b -> p (a b)"),
                                                    ALU.subtract).then_inc(q["p_lo"], 1)
                    if alive(t + 3):
                        dve.wait_ge(q["q_act"], 2 * t + 8)
                        positive_wait(dve, q["s_ps"], t + 2)
                        nc.vector.tensor_tensor(q_hl[:, par(3), 1, :], q_f[:, par(3), :], q_hl[:, par(3), 0, :],
                                                ALU.subtract).then_inc(q["q_lo"], 1)
                    if alive(t):
                        dve.wait_ge(q["y_ps"], t + 1)
                        nc.vector.scalar_tensor_tensor(x[:, t, :], ps[:, 6, P:2 * P], inv, x[:, t, :],
                                                       ALU.mult, ALU.add).then_inc(q["res"], 1)
                        dve.wait_ge(q["res"], t + 1)
                        statistics((2 * l + 1) * TILES + t, t, par(0))
                    if alive(t + 4):
                        dve.wait_ge(s["rs"], t + (5 + 2 * l * TILES))
                        positive_wait(dve, q["xt_ps"], t + 3)
                        nc.vector.tensor_scalar(xhat[:, par(4), :], x[:, t + 4, :], mv[:, t + 4, 0:1],
                                                rstd[:, t + 4:t + 5] if isinstance(t, int) else rstd[:, bass.ds(t + 4, 1)],
                                                ALU.subtract, ALU.mult).then_inc(q["xh"], 1)

                pipeline(dve, step, TILES, 0, 4)

            def routing(l):
                q = F[l]
                nc.vector.memset(comb16[:, :, :], 0.0).then_inc(q["c16"], 1)
                for g in range(GROUPS):
                    if g >= 2:
                        dve.wait_ge(q["xt_ps"], g - 1)
                    for t in range(G * g, G * g + G):
                        dve.wait_ge(s["rs"], t + (1 + (2 * l + 1) * TILES))
                        nc.vector.tensor_scalar(fx[:, g % 2, (t % G) * P:(t % G + 1) * P], x[:, t, :], mv[:, t, 0:1], rstd[:, t:t + 1],
                                                ALU.subtract, ALU.mult).then_inc(q["xh"], 1)
                    if g >= 1:
                        low(q, g - 1)
                low(q, GROUPS - 1)
                dve.wait_ge(q["lg_ps"], 1)
                nc.vector.tensor_scalar(logits, ps[:, 4, 0:TILES * EXPERTS].rearrange("p (t e) -> p t e", e=EXPERTS),
                                        1 / WSCALE, None, ALU.mult).then_inc(q["lg"], 1)
                dve.wait_ge(q["lg"], 1)
                for t in range(TILES):
                    nc.vector.max(top_v[:, t, :], logits[:, t, :]).then_inc(q["top"], 1)
                for t in range(TILES):
                    dve.wait_ge(q["top"], t + 1)
                    nc.vector.max_index(top_i[:, t, :], top_v[:, t, :], logits[:, t, :]).then_inc(q["idx"], 1)
                nc.vector.tensor_tensor(diff, top_v[:, :, 1], top_v[:, :, 0], ALU.subtract).then_inc(q["dif"], 1)
                dve.wait_ge(q["idx"], TILES)
                nc.vector.tensor_copy(top_f, top_i[:, :, 0:2]).then_inc(q["idx"], 1)
                dve.wait_ge(q["idx"], TILES + 1)
                dve.wait_ge(s["cst"], 48)
                for c in range(2):
                    nc.vector.tensor_tensor(one_hot[:, c, :, :], iota8[:, :].unsqueeze(1).broadcast_to([P, TILES, EXPERTS]),
                                            top_f[:, :, c:c + 1].broadcast_to([P, TILES, EXPERTS]), ALU.is_equal).then_inc(q["oh"], 1)
                dve.wait_ge(q["ex"], 1)
                nc.vector.tensor_scalar(diff, prob[:, :, 1], 1.0, None, ALU.add).then_inc(q["pr"], 1)
                dve.wait_ge(q["pr"], 1)
                nc.vector.reciprocal(prob[:, :, 0], diff).then_inc(q["pr"], 1)
                dve.wait_ge(q["pr"], 2)
                nc.vector.tensor_tensor(prob[:, :, 1], prob[:, :, 1], prob[:, :, 0], ALU.mult).then_inc(q["pr"], 1)
                dve.wait_ge(q["pr"], 3)
                dve.wait_ge(q["oh"], 2)
                for c in range(2):
                    nc.vector.tensor_tensor(one_hot[:, c, :, :], one_hot[:, c, :, :],
                                            prob[:, :, c:c + 1].broadcast_to([P, TILES, EXPERTS]), ALU.mult).then_inc(q["oh"], 1)
                dve.wait_ge(q["oh"], 4)
                nc.vector.tensor_tensor(comb, one_hot[:, 0, :, :], one_hot[:, 1, :, :], ALU.add).then_inc(q["cb"], 1)
                dve.wait_ge(q["cb"], 1)
                dve.wait_ge(q["c16"], 1)
                for col in (HI_ROW, HI2_ROW):
                    nc.vector.tensor_copy(comb16[:, :, col:col + EXPERTS], comb).then_inc(q["c16"], 1)
                dve.wait_ge(q["c16"], 3)
                nc.vector.tensor_tensor(comb16[:, :, LO_ROW:LO_ROW + EXPERTS], comb, comb16[:, :, HI_ROW:HI_ROW + EXPERTS],
                                        ALU.subtract).then_inc(q["c16"], 1)
                dve.wait_ge(q["ct_ps"], 1)
                nc.vector.tensor_copy(combT[:, tokens // 2:tokens], half_bank[3]).then_inc(q["ct_lo"], 1)

            def low(q, g):
                dve.wait_ge(q["xt_hi"], g + 1)
                r = slice(g * GT, (g + 1) * GT)
                nc.vector.tensor_tensor(xTa[:, 1, r], ps[:, g % 2, :], xTa[:, 0, r], ALU.subtract).then_inc(q["xt_lo"], 1)

            def experts0():
                q = F[0]
                with dve.Fori(0, GROUPS // 2) as i:
                    for k in range(2 * STEPS0):
                        n = 2 * STEPS0 * i + k
                        u = k % 2
                        dve.wait_ge(q["act"], n + 1)
                        if k >= 2:
                            dve.wait_ge(q["gt"], n - 1)
                        nc.vector.scalar_tensor_tensor(act_f[:, u, :], ps[:, 2 + u, :], 1 / WSCALE, act_f[:, u, :],
                                                       ALU.mult, ALU.mult).then_inc(q["t1"], 1)
                        dve.wait_ge(q["t1"], n + 1)
                        if k >= 2:
                            dve.wait_ge(q["lo"], n - 1)
                        nc.vector.tensor_tensor(gated[:, u, :], ps[:, 4 + u, :], act_f[:, u, :], ALU.mult).then_inc(q["gt"], 1)
                        if k == STEPS0 + 3:
                            residual0(i, 0)
                    residual0(i, 1)

            def residual0(i, half):
                q = F[0]
                gi = 2 * i + half
                dve.wait_ge(q["down"], 2 * STEPS0 * i + STEPS0 * (half + 1))
                nc.vector.scalar_tensor_tensor(
                    x[:, bass.ds(8 * i + 4 * half, G), :].rearrange("p t d -> p (t d)"), ps[:, 6 + half, :], 1 / WSCALE,
                    x[:, bass.ds(8 * i + 4 * half, G), :].rearrange("p t d -> p (t d)"), ALU.mult, ALU.add).then_inc(q["res"], 1)
                dve.wait_ge(q["res"], gi + 1)
                for t in range(G):
                    statistics(2 * TILES + 8 * i + 4 * half + t, 8 * i + (4 * half + t), t % 2)

            def experts1():
                q = F[1]
                for g in range(GROUPS):
                    dve.wait_ge(q["b2_ps"], g + 1)
                    r = x[:, G * g:G * (g + 1), :].rearrange("p t d -> p (t d)")
                    nc.vector.scalar_tensor_tensor(r, ps[:, 4 + g % 2, :], 1 / WSCALE, r, ALU.mult, ALU.add).then_inc(q["b2_r"], 1)
                dve.wait_ge(q["c16"], 4)
                nc.vector.tensor_scalar(comb, comb, 1 / WSCALE, None, ALU.mult).then_inc(q["cb"], 1)
                dve.wait_ge(q["cb"], 2)
                dve.wait_ge(q["b2_r"], GROUPS)
                K = GROUPS * STEPS1
                with dve.Fori(0, EXPERTS) as e:
                    for k in range(K):
                        n = K * e + k
                        u = k % 2
                        dve.wait_ge(q["hi"], n + 1)
                        if k >= 2:
                            dve.wait_ge(q["down"], n - 1)
                        nc.vector.tensor_tensor(hid[:, u, 1, :], act_f[:, u, :], hid[:, u, 0, :], ALU.subtract).then_inc(q["lo"], 1)
                        if k % STEPS1 == 2 and k >= STEPS1:
                            accumulate(e, k // STEPS1 - 1)
                    accumulate(e, GROUPS - 1)

            def accumulate(e, g):
                q = F[1]
                dve.wait_ge(q["down"], GROUPS * STEPS1 * e + STEPS1 * (g + 1))
                for t in range(G):
                    ins = nc.vector.scalar_tensor_tensor(x[:, G * g + t, :], ps[:, 4 + g % 2, t * P:(t + 1) * P],
                                                         comb[:, G * g + t, bass.ds(e, 1)], x[:, G * g + t, :], ALU.mult, ALU.add)
                ins.then_inc(q["res"], 1)

            keys_values(0)
            attention(0)
            routing(0)
            experts0()
            keys_values(1)
            attention(1)
            routing(1)
            experts1()

        @block.tensor
        def _(pe):
            def three(dst, lhs, rhs, start=True, stop=True, **kw):
                pe.matmul(dst, lhs[0], rhs[0], start=start, stop=False, **kw)
                pe.matmul(dst, lhs[0], rhs[1], start=False, stop=False, **kw)
                return pe.matmul(dst, lhs[1], rhs[0], start=False, stop=stop, **kw)

            pe.wait_ge(s["ids"], 16)
            pe.wait_ge(s["ld_w"], 16 * 8)
            for h in range(2):
                for n in range(4):
                    mm = pe.transpose(ps[:, h, n * P:(n + 1) * P], w_raw[:, 4 * h + n, :], ident[:, :])
                mm.then_inc(s["wt_ps"], 1)
            pe.wait_ge(s["ld_k"], 16 * 5)
            pe.transpose(ps[:, 6, 0:P], col_raw[:, :], ident[:, :]).then_inc(s["col_ps"], 1)
            pe.wait_ge(s["ld_c"], 16 * GROUPS)
            for g in range(GROUPS):
                for n in range(G):
                    mm = pe.transpose(ps[:, 2 + g, n * P:(n + 1) * P], ctx_raw[:, G * g + n, :], ident[:, :])
                mm.then_inc(s["ct_ps"], 1)
            pe.wait_ge(s["wt_lo"], 2)
            pe.wait_ge(s["ct_lo"], GROUPS)
            pe.wait_ge(s["bias_l"], 1)
            pe.wait_ge(s["cst"], 48)

            def W(l, which):
                n = 4 * l + "qkvo".index(which)
                return wT[:, 0, n, :], wT[:, 1, n, :]

            def keys_values(l):
                q = KV[l]
                for g in range(GROUPS):
                    if g >= 2:
                        pe.wait_ge(q["k_f"], g - 1)
                    r = slice(g * GT, (g + 1) * GT)
                    three(ps[:, g % 2, :], W(l, "k"), (ctx_T[:, 0, r], ctx_T[:, 1, r])).then_inc(q["k_ps"], 1)
                wv = W(l, "v")
                for j in range(TILES // 2):
                    if j >= 2:
                        pe.wait_ge(q["v_f"], j - 1)
                    for n in range(4):
                        c = [ctx_T[:, i, (4 * j + n) * SEQ:(4 * j + n + 1) * SEQ] for i in range(2)]
                        cols_n = slice(n * P, (n + 1) * P)
                        pe.matmul(ps[:, 4 + j % 2, cols_n], two_rows[:, :], bias_rows[:, 2 * l, :], start=True, stop=False)
                        for ci, wi in ((0, 0), (0, 1), (1, 0)):
                            for h2 in range(2):
                                mm = pe.matmul(ps[64 * h2:64 * h2 + 64, 4 + j % 2, cols_n], c[ci], wv[wi], start=False, stop=(ci == 1))
                    mm.then_inc(q["v_ps"], 1)

            def attention(l):
                q = A[l]
                pe.wait_ge(KV[l]["v_w"], 4 * (TILES // 2))

                def step(t, u):
                    par = lambda k: (u + k) % 2 if not isinstance(t, int) else (t + k) % 2
                    if alive(t + 2):
                        pr = par(2)
                        pe.wait_ge(q["q_lo"], t + 3)
                        if isinstance(t, int):
                            pe.wait_ge((q["kb0"], q["kb1"])[pr], 256 * ((t + 2) // 2 + 1))
                        else:
                            pe.wait_ge((q["kb0"], q["kb1"])[pr], 128 * t + (512 - 128 * u))
                        positive_wait(pe, q["sub"], t + 2)
                        for qi, ki in ((0, 0), (0, 1), (1, 0)):
                            for h in range(2):
                                for b in range(PER_TILE):
                                    mm = pe.matmul(ps[64 * b:64 * b + 64, h, :], q_hl[:, pr, qi, 64 * b:64 * b + 64],
                                                   k_blocks[:, pr, ki, b, 512 * h:512 * h + 512],
                                                   start=(qi + ki == 0), stop=(qi == 1))
                        mm.then_inc(q["s_ps"], 1)
                    if alive(t + 3):
                        pe.wait_ge(q["xh"], t + 4)
                        positive_wait(pe, q["q_act"], 2 * t + 6)
                        pe.transpose(ps[:, 4, 0:P], xhat[:, par(3), :], ident[:, :]).then_inc(q["xt_ps"], 1)
                    if alive(t):
                        pe.wait_ge(q["on"], 2 * t + 2)
                        positive_wait(pe, q["res"], t)
                        pe.transpose(ps[:, 6, 0:P], o_n[:, par(0), :], ident[:, :]).then_inc(q["ot_ps"], 1)
                    if alive(t + 1):
                        pe.wait_ge(q["ex"], t + 2)
                        for h in range(2):
                            positive_wait(pe, q["p_lo"], 2 * t + (1 + h))
                            for n in range(4):
                                c = (4 * h + n) * P
                                mm = pe.transpose(ps[:, 2 + h, n * P:(n + 1) * P], probs[:, par(1), c:c + P], ident[:, :])
                            mm.then_inc(q["p_ps"], 1)
                    if alive(t + 3):
                        pe.wait_ge(q["xt_hi"], t + 4)
                        pe.wait_ge(q["xt_lo"], t + 4)
                        three(ps[:, 4, P:2 * P], W(l, "q"), (xT[:, par(3), 0, :], xT[:, par(3), 1, :])).then_inc(q["q_ps"], 1)
                    if alive(t):
                        pe.wait_ge(q["ot_hi"], t + 1)
                        pe.wait_ge(q["ot_lo"], t + 1)
                        dst = ps[:, 6, P:2 * P]
                        three(dst, (oT[:, par(0), 0, :], oT[:, par(0), 1, :]), W(l, "o"), stop=False)
                        pe.matmul(dst, two_rows[:, :], bias_rows[:, 2 * l + 1, :], start=False, stop=True).then_inc(q["y_ps"], 1)
                    if alive(t + 1):
                        positive_wait(pe, q["on"], 2 * t + 2)
                        pe.wait_ge(q["p_lo"], 2 * t + 4)
                        for n in range(PAIRS):
                            w = PER_TILE * 2 * VW
                            v = [vals[:, t + 1, i, n, :, :, :].rearrange("p b h v -> p (b h v)") for i in range(2)]
                            mm = three(ps[:, 5, n * w:(n + 1) * w], (pT[:, par(1), 0, n, :], pT[:, par(1), 1, n, :]), v)
                        mm.then_inc(q["o_ps"], 1)

                pipeline(pe, step, TILES, 0, 4)

            def routing(l):
                q = F[l]
                pe.wait_ge(A[l]["res"], TILES)
                pe.wait_ge(s["gate_l"], 2)
                for g in range(GROUPS):
                    if g >= 2:
                        pe.wait_ge(q["xt_lo"], g - 1)
                    for n in range(G):
                        pe.wait_ge(q["xh"], G * g + n + 1)
                        mm = pe.transpose(ps[:, g % 2, n * P:(n + 1) * P], fx[:, g % 2, n * P:(n + 1) * P], ident[:, :])
                    mm.then_inc(q["xt_ps"], 1)
                for t in range(TILES):
                    pe.wait_ge(q["xt_lo"], t // G + 1)
                    r = slice(t * P, (t + 1) * P)
                    mm = three(ps[:, 4, t * EXPERTS:(t + 1) * EXPERTS], (xTa[:, 0, r], xTa[:, 1, r]),
                               (gate_w[:, l, 0, :], gate_w[:, l, 1, :]))
                mm.then_inc(q["lg_ps"], 1)
                pe.wait_ge(q["c16"], 4)
                for t in range(TILES):
                    c = (t % 8) * P
                    mm = pe.transpose(half_bank[2 + t // 8][:, c:c + P], comb16[:, t, :], ident16[:, :])
                mm.then_inc(q["ct_ps"], 1)
                pe.wait_ge(q["ct_hi"], 1)
                pe.wait_ge(q["ct_lo"], 1)

            def down(dst, h, w, first, last):
                for t in range(G):
                    r = slice(t * P, (t + 1) * P)
                    mm = three(dst[:, r], (h[:, 0, r], h[:, 1, r]), w, start=first and t == 0, stop=last, skip_group_check=True)
                return mm

            def experts0():
                q = F[0]
                pe.wait_ge(s["ch_lo"], CHUNKS0)
                K = 2 * STEPS0
                with pe.Fori(0, GROUPS // 2) as i:
                    for k in range(K + 2):
                        if k < K:
                            n = K * i + k
                            f = slice((k % STEPS0) * P, (k % STEPS0 + 1) * P)
                            tok = bass.ds(1024 * i + GT * (k // STEPS0), GT)
                            xs = (xTa[:, 0, tok], xTa[:, 1, tok])
                            if k >= 2:
                                pe.wait_ge(q["gt"], n - 1)
                            three(ps[:, k % 2, :], (wg[:, 0, f], wg[:, 1, f]), xs)
                            three(ps[:, 2 + k % 2, :], (wu[:, 0, f], wu[:, 1, f]), xs)
                            pe.matmul(ps[:, 4 + k % 2, :], expert_rows[:, f], combT[:, tok], start=True, stop=True).then_inc(q["up"], 1)
                        if k >= 2:
                            j = k - 2
                            pe.wait_ge(q["lo"], K * i + (j + 1))
                            if j == 0:
                                pe.wait_ge(s["st"], 2 * TILES + 8 * i)
                            half, f = divmod(j, STEPS0)
                            down(ps[:, 6 + half, :], hid[:, j % 2, :, :],
                                 (wd[:, 0, f * P:(f + 1) * P], wd[:, 1, f * P:(f + 1) * P]), f == 0, f == STEPS0 - 1).then_inc(q["down"], 1)

            def experts1():
                q = F[1]
                pe.wait_ge(s["b2l"], 1)
                for g in range(GROUPS):
                    if g >= 2:
                        pe.wait_ge(q["b2_r"], g - 1)
                    for t in range(G):
                        r = slice((G * g + t) * P, (G * g + t + 1) * P)
                        mm = pe.matmul(ps[:, 4 + g % 2, t * P:(t + 1) * P], combT[:, r], b2_rows[:, :], start=True, stop=True)
                    mm.then_inc(q["b2_ps"], 1)
                pe.wait_ge(q["b2_r"], GROUPS)
                pe.wait_ge(s["ch_lo"], len(chunks))
                K = GROUPS * STEPS1
                with pe.Fori(0, EXPERTS) as e:
                    for k in range(K + 2):
                        if k < K:
                            g, f = divmod(k, STEPS1)
                            fs = slice(f * P, (f + 1) * P)
                            r = slice(g * GT, (g + 1) * GT)
                            if k >= 4:
                                pe.wait_ge(q["act"], K * e + (k - 3))
                            three(ps[:, k % 4, :], (w1[:, 0, e, fs], w1[:, 1, e, fs]),
                                  (xTa[:, 0, r], xTa[:, 1, r])).then_inc(q["up"], 1)
                        if k >= 2:
                            j = k - 2
                            g, f = divmod(j, STEPS1)
                            pe.wait_ge(q["lo"], K * e + (j + 1))
                            if f == 0 and g >= 2:
                                pe.wait_ge(q["res"], GROUPS * e + (g - 1))
                            down(ps[:, 4 + g % 2, :], hid[:, j % 2, :, :], (w2[:, 0, e, f, :], w2[:, 1, e, f, :]),
                                 f == 0, f == STEPS1 - 1).then_inc(q["down"], 1)
                    pe.wait_ge(q["res"], GROUPS * e + GROUPS)

            keys_values(0)
            attention(0)
            routing(0)
            experts0()
            pe.wait_ge(F[0]["res"], GROUPS)
            keys_values(1)
            attention(1)
            routing(1)
            experts1()


def constants():
    rows = np.zeros((P, HID0), np.float16)
    for r in (HI_ROW, LO_ROW):
        rows[r + np.arange(HID0) // M0, np.arange(HID0)] = 1
    two = np.zeros((P, P), np.float16)
    two[[0, 32]] = 1
    return {"ident": np.eye(P, dtype=np.float32), "expert_rows": rows, "two_rows": two,
            "iota8": np.broadcast_to(np.arange(EXPERTS, dtype=np.float32), (P, EXPERTS)).copy()}


def kernel(**inputs):
    import concourse.bacc as bacc
    from concourse.bass_utils import run_bass_kernel_spmd

    nc = bacc.Bacc("TRN2", target_bir_lowering=False, num_devices=1)
    arrays, args = {}, {}
    for name, value in {**inputs, **constants()}.items():
        v = np.ascontiguousarray(value)
        arrays[f"in_{name}"] = v
        args[name] = nc.dram_tensor(f"in_{name}", v.shape, mybir.dt.from_np(v.dtype), kind="ExternalInput").ap()
    out = nc.dram_tensor("out", inputs["x"].shape, F32, kind="ExternalOutput").ap()
    build(nc, args, out)
    r = run_bass_kernel_spmd(nc, [arrays], core_ids=[0])
    return r.results[0]["out"]
```

```python
from contextlib import ExitStack

import numpy as np

import concourse.bass as bass
from concourse import mybir

F32 = mybir.dt.float32
F16 = mybir.dt.float16
U32 = mybir.dt.uint32
ALU = mybir.AluOpType
ACT = mybir.ActivationFunctionType
AX = mybir.AxisListType

P = 128
SEQ = 64
PER_TILE = P // SEQ
D = 128
HEADS = 16
HD = D // HEADS
PAIRS = HEADS // 2
QUADS = 4
QUAD = HEADS // QUADS
HALF = HEADS * SEQ // 2
VW = HD + 1
EXPERTS = 8
M0 = 176
M1 = 512
HID0 = EXPERTS * M0
STEPS0 = HID0 // P
STEPS1 = M1 // P
G = 4
EPS = 1e-5
WSCALE = 1024.0
HI_ROW, LO_ROW, HI2_ROW = 0, 32, 64


def positive_wait(eng, sem, value):
    if not isinstance(value, int) or value > 0:
        eng.wait_ge(sem, value)


def pipeline(eng, step, tiles, ahead):
    first = 2
    last = (tiles - ahead - first) // 2 * 2 + first
    for t in range(-ahead, first):
        step(t, 0)
    with eng.Fori(0, (last - first) // 2) as i:
        step(2 * i + first, 0)
        step(2 * i + (first + 1), 1)
    for t in range(last, tiles + 1):
        step(t, 0)


def build(nc, a, out):
    tokens = a["x"].shape[0] * a["x"].shape[1]
    TILES = tokens // P
    GROUPS = TILES // G
    GT = G * P

    with ExitStack() as ctx:
        def sb(name, shape, dt):
            return ctx.enter_context(nc.sbuf_tensor(name, shape, dt))

        def sems(names, suffix=""):
            return {n: ctx.enter_context(nc.semaphore(n + suffix)) for n in names.split()}

        x = sb("x_res", [P, TILES, D], F32)
        mv = sb("mean_var", [P, TILES, 2], F32)
        rstd = sb("rstd", [P, TILES], F32)
        mv_now = sb("mv_now", [P, G, 2], F32)
        zero_eps = sb("zero_eps", [P, 2], F32)
        b1_now = sb("b1_now", [P, STEPS1], F32)
        minus_half = sb("minus_half", [P, 1], F32)
        stats = sb("stats", [P, G, 6], F32)
        wait_carrier = sb("wait_carrier", [P, 2], F32)
        ident = sb("ident", [P, P], F32)
        ident16 = sb("ident16", [P, P], F16)
        iota8 = sb("iota8", [P, EXPERTS], F32)
        expert_rows = sb("expert_rows", [P, HID0], F16)
        two_rows = sb("two_rows", [P, P], F16)
        w_raw = sb("w_raw", [P, 8, P], F32)
        wT = sb("wT", [P, 2, 8, P], F16)
        col_raw = sb("col_raw", [P, P], F32)
        cols = sb("cols", [P, P], F32)
        N_B1 = EXPERTS * STEPS1
        bias_col = cols[:, N_B1:N_B1 + 4]
        b1_col = cols[:, 0:N_B1].rearrange("p (e j) -> p e j", j=STEPS1)
        bias_raw = sb("bias_raw", [33, 4, P], F32)
        bias_hi = sb("bias_hi", [33, 4, P], F16)
        bias_rows = sb("bias_rows", [P, 4, P], F16)
        gate_raw = sb("gate_raw", [P, 2, EXPERTS], F32)
        gate_w = sb("gate_w", [P, 2, 2, EXPERTS], F16)
        b2_raw = sb("b2_raw", [P, D], F32)
        b2_hi = sb("b2_hi", [P, D], F16)
        b2_rows = sb("b2_rows", [P, D], F16)
        ctx_T = sb("ctx_T", [P, 2, tokens], F16)
        keys = sb("keys", [P, TILES, 2, PER_TILE, QUAD, SEQ], F16)
        keys_now = sb("keys_now", [P, 2, 2, PER_TILE, QUAD * SEQ], F16)
        q_blk = sb("q_blk", [P, 2, 2, QUADS, P], F16)
        wk_m = sb("wk_m", [P, 2, 2, QUAD, P], F16)
        quad_mask = sb("quad_mask", [P, QUAD], F32)
        bk_m = sb("bk_m", [P, 2, QUAD], F32)
        vals = sb("vals", [P, TILES, 2, PAIRS, PER_TILE, 2, VW], F16)
        vals_now = sb("vals_now", [P, 2, 2, PAIRS, PER_TILE * 2 * VW], F16)
        wg = sb("wg", [P, 2, HID0], F16)
        wu = sb("wu", [P, 2, HID0], F16)
        wd = sb("wd", [P, 2, HID0], F16)
        w12 = sb("w12", [P, 2, 8, 1024], F16)
        w1 = w12[:, :, 0:4, :].rearrange("p i c (e f) -> p i (c e) f", f=M1)
        w2 = w12[:, :, 4:8, :].rearrange("p i c (e j d) -> p i (c e) j d", j=STEPS1, d=D)
        w_stage = sb("w_stage", [P, 2, HID0], F32)
        area = sb("area", [P, 12400], F32)
        used = [0]

        def carve(shape, dt):
            n = int(np.prod(shape)) * (2 if dt == F16 else 4) // 4
            ap = area[:, used[0]:used[0] + n]
            used[0] += n
            assert used[0] <= 12400, used
            if dt == F16:
                ap = ap.bitcast(F16)
            names = "abcd"[:len(shape)]
            if len(shape) > 1:
                ap = ap.rearrange(f"p ({' '.join(names)}) -> p {' '.join(names)}", **dict(zip(names[1:], shape[1:])))
            return ap

        xhat = carve([2, P], F32)
        xT = carve([2, 2, P], F16)
        q_f = carve([2, P], F32)
        mx = carve([2, HEADS], F32)
        probs = carve([2, HEADS * SEQ], F32)
        pT = carve([2, 2, PAIRS, P], F16)
        p_f = carve([2, 4 * P], F32)
        rden = carve([2, HEADS], F32)
        o_n = carve([2, P], F32)
        oT = carve([2, 2, P], F16)
        used[0] = 0
        ctx_raw = carve([TILES, D], F32)
        k_f = carve([2, GT], F32)
        v_f = carve([2, GT], F32)
        used[0] = 0
        fx = carve([2, G * P], F32)
        xTa = carve([2, tokens], F16)
        logits = carve([TILES, EXPERTS], F32)
        top_v = carve([TILES, 8], F32)
        top_i = carve([TILES, 8], F32).bitcast(U32)
        top_f = carve([TILES, 2], F32)
        diff = carve([TILES], F32)
        prob = carve([TILES, 2], F32)
        one_hot = carve([2, TILES, EXPERTS], F32)
        comb = carve([TILES, EXPERTS], F32)
        comb16 = carve([TILES, P], F16)
        combT = carve([tokens], F16)
        act_f = carve([4, GT], F32)
        gated = carve([4, GT], F32)
        hid = carve([4, 2, GT], F16)

        ps = ctx.enter_context(nc.psum_tensor("ps", [P, 8, 512], F32))
        half_bank = [ps[:, b, :].bitcast(F16) for b in range(8)]

        s = sems("ld_x0 ld_x1 ld_x2 ld_x3 ld_c ld_w ld_k ld_s col_ps cols ids ones cast16 wt_ps wt_hi wt_lo ct_ps ct_hi ct_lo small_hi small_lo "
                 "zero vone mh st agg ag rs out_d "
                 "ch_in0 ch_in1 ch_hi ch_lo cst msk bkm")
        KV = [sems("k_ps k_f k_hi k_lo v_ps v_f v_w", f"_kv{l}") for l in range(2)]
        A = [sems("vb0 vb1 p_f p_lop kb0 kb1 xh xt_ps xt_hi xt_lo q_ps q_act q_lo s_ps mx sub ex p_ps p_hi p_lo o_ps rd on "
                  "ot_ps ot_hi ot_lo y_ps res", f"_a{l}") for l in range(2)]
        F = [sems("xh xt_ps xt_hi xt_lo lg_ps lg top idx dif ex pr oh cb c16 ct_ps ct_hi ct_lo "
                  "up act hi lo down res " + ("t1 gt", "b1 b2_ps b2_r")[l], f"_f{l}") for l in range(2)]

        CHUNKS0 = 3
        w_in = [a["L0_ffn_w_g"].rearrange("e d m -> d e m"), a["L0_ffn_w_u"].rearrange("e d m -> d e m"),
                a["L0_ffn_w_d"].rearrange("e m d -> (e m) d").rearrange("(j p) d -> p j d", p=P)]
        w_out = [wg, wu, wd]
        chunks = w_in
        chunks += [a["L1_ffn_W1"][e:e + 2].rearrange("e d f -> d e f") for e in range(0, EXPERTS, 2)]
        chunks += [a["L1_ffn_W2"][e:e + 2].rearrange("e (j p) d -> p (e j) d", p=P) for e in range(0, EXPERTS, 2)]
        CHUNK1 = 2 * M1
        CHUNK_STEPS = (2, 7, 12, 17)
        x_dram = a["x"].rearrange("b s d -> (b s) d").rearrange("(t p) d -> p t d", p=P)
        c_dram = a["ctx_1024"].rearrange("b s d -> (b s) d").rearrange("(t p) d -> p t d", p=P)
        out_dram = out.rearrange("b s d -> (b s) d").rearrange("(t p) d -> p t d", p=P)
        W_NAMES = [f"L{l}_xattn_W{n}" for l in range(2) for n in "qkvo"]

        def alive(t):
            return not isinstance(t, int) or 0 <= t < TILES

        def within(count):
            return min(count, TILES) if isinstance(count, int) else count

        block = ctx.enter_context(nc.Block())

        @block.sync
        def _(sp):
            sp.dma_start(ident[:, :], a["ident"]).then_inc(s["ids"], 16)
            for n, name in enumerate(W_NAMES):
                sp.dma_start(w_raw[:, n, :], a[name]).then_inc(s["ld_w"], 16)
            for g in range(GROUPS):
                sp.dma_start(ctx_raw[:, G * g:G * (g + 1), :], c_dram[:, G * g:G * (g + 1), :]).then_inc(s["ld_c"], 16)
            sp.dma_start(iota8[:, :], a["iota8"]).then_inc(s["cst"], 16)
            sp.dma_start(expert_rows[:, :], a["expert_rows"]).then_inc(s["cst"], 16)
            sp.dma_start(two_rows[:, :], a["two_rows"]).then_inc(s["cst"], 16)
            sp.dma_start(quad_mask[:, :], a["quad_mask"]).then_inc(s["cst"], 16)

            def load_chunk(c):
                src = chunks[c]
                n = src.shape[1] * src.shape[2]
                dst = w_stage[:, c % 2, 0:n].rearrange("p (a b) -> p a b", b=src.shape[2])
                sp.dma_start(dst, src).then_inc((s["ch_in0"], s["ch_in1"])[c % 2], 16)

            load_chunk(0)
            load_chunk(1)
            sp.wait_ge(s["ch_lo"], 1)
            load_chunk(2)

            def attention_operands(l):
                q = A[l]

                def tile_keys(t, par):
                    sp.dma_start(keys_now[:, par, :, :, :].rearrange("p a b k -> p (a b k)"),
                                 keys[:, t, :, :, :, :].rearrange("p a b j k -> p (a b j k)")).then_inc((q["kb0"], q["kb1"])[par], 16)

                def tile_vals(t, par):
                    sp.dma_start(vals_now[:, par, :, :, :].rearrange("p a b v -> p (a b v)"),
                                 vals[:, t, :, :, :, :, :].rearrange("p a n b h v -> p (a n b h v)")).then_inc((q["vb0"], q["vb1"])[par], 16)

                sp.wait_ge(KV[l]["k_lo"], GROUPS * QUAD)
                if l == 1:
                    sp.wait_ge(A[0]["s_ps"], 2 * TILES)
                    sp.wait_ge(A[0]["o_ps"], TILES)
                tile_keys(0, 0)
                tile_keys(1, 1)
                sp.wait_ge(KV[l]["v_w"], 4 * (TILES // 2))
                for u in range(2):
                    sp.wait_ge(q["s_ps"], 2 * u + 2)
                    tile_keys(2 + u, u)
                    tile_vals(u, u)
                with sp.Fori(2, TILES // 2) as i:
                    for u in range(2):
                        sp.wait_ge(q["s_ps"], 4 * i + (2 * u - 2))
                        tile_keys(2 * i + u, u)
                        sp.wait_ge(q["o_ps"], 2 * i + (u - 3))
                        tile_vals(2 * i + (u - 2), u)
                for t in range(TILES - 2, TILES):
                    sp.wait_ge(q["o_ps"], t - 1)
                    tile_vals(t, t % 2)

            attention_operands(0)
            for c in range(3, len(chunks)):
                sp.wait_ge(s["ch_lo"], c - 1)
                load_chunk(c)
            attention_operands(1)
            for g in range(GROUPS):
                sp.wait_ge(F[1]["res"], (EXPERTS - 1) * GROUPS + g + 1)
                sp.dma_start(out_dram[:, G * g:G * (g + 1), :], x[:, G * g:G * (g + 1), :]).then_inc(s["out_d"], 16)
            sp.wait_ge(s["out_d"], 16 * GROUPS)

        @block.scalar
        def _(act):
            act.wait_ge(s["ones"], 1)
            for g in range(GROUPS):
                act.dma_start(x[:, G * g:G * (g + 1), :], x_dram[:, G * g:G * (g + 1), :]).then_inc((s["ld_x0"], s["ld_x1"], s["ld_x2"], s["ld_x3"])[g], 16)
            for n, name in enumerate(["L0_xattn_bq", "L0_xattn_bk", "L1_xattn_bq", "L1_xattn_bk"]):
                act.dma_start(col_raw[N_B1 + n:N_B1 + n + 1, :], a[name].rearrange("(o p) -> o p", o=1)).then_inc(s["ld_k"], 16)
            act.dma_start(col_raw[0:N_B1, :], a["L1_ffn_b1"].rearrange("e (j p) -> (e j) p", p=P)).then_inc(s["ld_k"], 16)
            for n, name in enumerate(["L0_xattn_bv", "L0_xattn_bo", "L1_xattn_bv", "L1_xattn_bo"]):
                for r in (0, 32):
                    act.dma_start(bias_raw[r:r + 1, n, :], a[name].rearrange("(o p) -> o p", o=1)).then_inc(s["ld_s"], 16)
            act.dma_start(gate_raw[:, 0, :], a["L0_ffn_w_gate"]).then_inc(s["ld_s"], 16)
            act.dma_start(gate_raw[:, 1, :], a["L1_ffn_gate_w"]).then_inc(s["ld_s"], 16)
            for r in (HI_ROW, LO_ROW, HI2_ROW):
                act.dma_start(b2_raw[r:r + EXPERTS, :], a["L1_ffn_b2"]).then_inc(s["ld_s"], 16)

            act.wait_ge(s["col_ps"], 1)
            nc.scalar.activation(cols[:, :], ps[:, 6, 0:P], ACT.Copy).then_inc(s["cols"], 1)
            for h in range(2):
                act.wait_ge(s["wt_ps"], h + 1)
                nc.scalar.activation(wT[:, 0, 4 * h:4 * h + 4, :], ps[:, h, :].rearrange("p (a b) -> p a b", a=4),
                                     ACT.Copy, scale=WSCALE).then_inc(s["wt_hi"], 1)
            for g in range(GROUPS):
                act.wait_ge(s["ct_ps"], g + 1)
                nc.scalar.activation(ctx_T[:, 0, g * GT:(g + 1) * GT], ps[:, 2 + g, :], ACT.Copy).then_inc(s["ct_hi"], 1)

            def split_high(c, hi):
                act.wait_ge((s["ch_in0"], s["ch_in1"])[c % 2], 16 * (c // 2 + 1))
                n = chunks[c].shape[1] * chunks[c].shape[2]
                nc.scalar.activation(hi, w_stage[:, c % 2, 0:n], ACT.Copy, scale=WSCALE).then_inc(s["ch_hi"], 1)

            for c in range(CHUNKS0):
                split_high(c, w_out[c][:, 0, :])

            def keys_values(l):
                q = KV[l]
                act.wait_ge(s["bkm"], 2)
                for g in range(GROUPS):
                    for j in range(QUAD):
                        n = QUAD * g + j
                        act.wait_ge(q["k_ps"], n + 1)
                        if n >= 2:
                            act.wait_ge(q["k_lo"], n - 1)
                        nc.scalar.activation(k_f[:, n % 2, :], ps[:, n % 2, :], ACT.Identity,
                                             bias=bk_m[:, l, j:j + 1], scale=1 / WSCALE).then_inc(q["k_f"], 1)
                        act.wait_ge(q["k_f"], n + 1)
                        nc.scalar.activation(keys[:, G * g:G * (g + 1), 0, :, j, :],
                                             k_f[:, n % 2, :].rearrange("p (t b k) -> p t b k", t=G, b=PER_TILE),
                                             ACT.Copy).then_inc(q["k_hi"], 1)
                for j in range(TILES // 2):
                    act.wait_ge(q["v_ps"], j + 1)
                    if j >= 2:
                        act.wait_ge(q["v_w"], 4 * (j - 1))
                    nc.scalar.activation(v_f[:, j % 2, :], ps[:, 4 + j % 2, :], ACT.Copy,
                                         scale=1 / WSCALE).then_inc(q["v_f"], 1)

            def attention(l):
                q = A[l]

                def step(t, u):
                    par = lambda k: (u + k) % 2 if not isinstance(t, int) else (t + k) % 2
                    if alive(t + 5):
                        act.wait_ge(q["xt_ps"], t + 6)
                        positive_wait(act, q["q_ps"], t + 4)
                        nc.scalar.activation(xT[:, par(5), 0, :], ps[:, 4, 0:P], ACT.Copy).then_inc(q["xt_hi"], 1)
                    if alive(t + 4):
                        act.wait_ge(q["q_ps"], t + 5)
                        positive_wait(act, q["q_lo"], QUADS * t + 3 * QUADS)
                        positive_wait(act, q["s_ps"], 2 * t + 6)
                        nc.scalar.activation(q_f[:, par(4), :], ps[:, 7, 0:P], ACT.Identity,
                                             bias=bias_col[:, 2 * l:2 * l + 1], scale=1 / WSCALE).then_inc(q["q_act"], 1)
                        for n in range(QUADS):
                            r = slice(32 * n, 32 * n + 32)
                            nc.scalar.activation(q_blk[r, par(4), 0, n, :], ps[r, 7, 0:P], ACT.Identity,
                                                 bias=bias_col[r, 2 * l:2 * l + 1], scale=1 / WSCALE).then_inc(q["q_act"], 1)
                    if alive(t + 3):
                        for h in range(2):
                            act.wait_ge(q["sub"], 2 * t + (7 + h))
                            r = slice(h * HALF, (h + 1) * HALF)
                            nc.scalar.activation(probs[:, par(3), r], probs[:, par(3), r], ACT.Exp,
                                                 scale=float(HD) ** -0.5).then_inc(q["ex"], 1)
                    if alive(t):
                        act.wait_ge(q["ot_ps"], t + 1)
                        positive_wait(act, q["y_ps"], t - 1)
                        nc.scalar.activation(oT[:, par(0), 0, :], ps[:, 6, 0:P], ACT.Copy).then_inc(q["ot_hi"], 1)
                    if alive(t + 2):
                        positive_wait(act, q["o_ps"], t + 1)
                        for h in range(2):
                            act.wait_ge(q["p_ps"], 2 * t + (5 + h))
                            nc.scalar.activation(pT[:, par(2), 0, 4 * h:4 * h + 4, :],
                                                 ps[:, 2 + h, :].rearrange("p (a b) -> p a b", a=4),
                                                 ACT.Copy).then_inc(q["p_hi"], 1)
                        positive_wait(act, q["p_lop"], t + 1)
                        nc.scalar.activation(p_f[:, par(2), :], ps[:, 3, :], ACT.Copy).then_inc(q["p_f"], 1)
                pipeline(act, step, TILES, 6)

            def routing(l):
                q = F[l]
                for g in range(GROUPS):
                    act.wait_ge(q["xt_ps"], g + 1)
                    nc.scalar.activation(xTa[:, 0, g * GT:(g + 1) * GT], ps[:, g % 2, :], ACT.Copy).then_inc(q["xt_hi"], 1)
                act.wait_ge(q["dif"], 1)
                nc.scalar.activation(prob[:, :, 1], diff, ACT.Exp).then_inc(q["ex"], 1)
                act.wait_ge(q["ct_ps"], 1)
                nc.scalar.activation(combT[:, 0:tokens // 2], half_bank[2], ACT.Copy).then_inc(q["ct_hi"], 1)

            def experts0():
                q = F[0]
                with act.Fori(0, GROUPS // 2) as i:
                    for k in range(2 * STEPS0 + 1):
                        n = 2 * STEPS0 * i + k
                        if k < 2 * STEPS0:
                            act.wait_ge(q["up"], n + 1)
                            if k >= 4:
                                act.wait_ge(q["gt"], n - 3)
                            nc.scalar.activation(act_f[:, k % 4, :], ps[:, k % 2, :], ACT.Silu,
                                                 scale=1 / WSCALE).then_inc(q["act"], 1)
                        if k >= 1:
                            act.wait_ge(q["gt"], n)
                            if k >= 5:
                                act.wait_ge(q["down"], n - 4)
                            nc.scalar.activation(hid[:, (k - 1) % 4, 0, :], gated[:, (k - 1) % 4, :],
                                                 ACT.Copy).then_inc(q["hi"], 1)
                        if k in CHUNK_STEPS:
                            m = CHUNK_STEPS.index(k)
                            act.wait_ge((s["ch_in0"], s["ch_in1"])[(CHUNKS0 + m) % 2], 32 * i + 16 * ((CHUNKS0 + m) // 2 + 1))
                            nc.scalar.activation(w12[:, 0, 4 * i + m, :], w_stage[:, (CHUNKS0 + m) % 2, 0:CHUNK1],
                                                 ACT.Copy, scale=WSCALE).then_inc(s["ch_hi"], 1)

            def experts1():
                q = F[1]
                K = GROUPS * STEPS1

                def expert(e):
                    nc.scalar.activation(b1_now[:, :], b1_col[:, e, :], ACT.Copy).then_inc(q["b1"], 1)
                    act.wait_ge(q["b1"], e + 1)
                    for k in range(K):
                        n = K * e + k
                        act.wait_ge(q["up"], n + 1)
                        positive_wait(act, q["lo"], n - 3)
                        nc.scalar.activation(act_f[:, k % 4, :], ps[:, k % 4, :], ACT.Gelu,
                                             bias=b1_now[:, k % STEPS1:k % STEPS1 + 1], scale=1 / WSCALE).then_inc(q["act"], 1)
                        act.wait_ge(q["act"], n + 1)
                        positive_wait(act, q["down"], n - 3)
                        nc.scalar.activation(hid[:, k % 4, 0, :], act_f[:, k % 4, :], ACT.Copy).then_inc(q["hi"], 1)

                expert(0)
                with act.Fori(1, EXPERTS) as e:
                    expert(e)

            keys_values(0)
            act.wait_ge(s["zero"], 2)
            attention(0)
            routing(0)
            experts0()
            act.wait_ge(F[0]["res"], GROUPS)
            keys_values(1)
            attention(1)
            act.wait_ge(s["ld_s"], 16 * (8 + 2 + 3))
            routing(1)
            experts1()

        @block.gpsimd
        def _(pool):
            nc.gpsimd.memset(minus_half[:, :], -0.5).then_inc(s["mh"], 1)
            nc.gpsimd.memset(wk_m[:, :, :, :, :], 0.0).then_inc(s["zero"], 1)
            nc.gpsimd.memset(q_blk[:, :, :, :, :], 0.0).then_inc(s["zero"], 1)

            def rstds(t, width, n, slot=0):
                pool.wait_ge(s["agg"], n + width)
                nc.gpsimd.tensor_tensor(mv[:, bass.ds(t, width), :], mv_now[:, slot:slot + width, :],
                                        zero_eps[:, :].unsqueeze(1).broadcast_to([P, width, 2]), ALU.add).then_inc(s["ag"], width)
                pool.wait_ge(s["ag"], n + width)
                nc.gpsimd.tensor_tensor(rstd[:, bass.ds(t, width)], mv[:, bass.ds(t, width), 1:2].rearrange("p a o -> p (a o)"),
                                        minus_half[:, 0:1].broadcast_to([P, width]), ALU.pow).then_inc(s["rs"], width)

            def attention(l):
                q = A[l]

                def step(t, u):
                    par = lambda k: (u + k) % 2 if not isinstance(t, int) else (t + k) % 2
                    if alive(t + 4):
                        pool.wait_ge(q["q_act"], 5 * t + 25)
                        positive_wait(pool, q["s_ps"], 2 * t + 6)
                        positive_wait(pool, q["p_lop"], t + 2)
                        for n in range(QUADS):
                            r = slice(32 * n, 32 * n + 32)
                            positive_wait(pool, q["q_lo"], QUADS * t + 4 * QUADS + n)
                            nc.gpsimd.tensor_tensor(q_blk[r, par(4), 1, n, :], q_f[r, par(4), :], q_blk[r, par(4), 0, n, :],
                                                    ALU.subtract).then_inc(q["q_lo"], 1)
                    if alive(t - 1):
                        pool.wait_ge(q["q_lo"], QUADS * within(t + 5))
                        rstds(t - 1, 1, t + ((2 * l + 1) * TILES - 1), par(1))
                    if alive(t + 2):
                        pool.wait_ge(q["p_f"], t + 3)
                        pool.wait_ge(q["p_hi"], 2 * t + 6)
                        positive_wait(pool, q["o_ps"], t + 1)
                        pool.wait_ge(q["q_lo"], QUADS * within(t + 5))
                        pool.wait_ge(s["rs"], max(t, 0) + (2 * l + 1) * TILES if isinstance(t, int) else t + (2 * l + 1) * TILES)
                        nc.gpsimd.tensor_tensor(pT[:, par(2), 1, 4:8, :].rearrange("p a b -> p (a b)"), p_f[:, par(2), :],
                                                pT[:, par(2), 0, 4:8, :].rearrange("p a b -> p (a b)"), ALU.subtract).then_inc(q["p_lop"], 1)

                pipeline(pool, step, TILES, 6)

            pool.wait_ge(s["mh"], 1)
            pool.wait_ge(s["zero"], 2)
            pool.wait_ge(s["ones"], 2)
            for g in range(GROUPS):
                rstds(G * g, G, G * g)
            attention(0)
            pool.wait_ge(s["rs"], 2 * TILES)
            q = F[0]
            with pool.Fori(0, GROUPS // 2) as i:
                for k in range(2 * STEPS0):
                    n = 2 * STEPS0 * i + k
                    pool.wait_ge(q["hi"], n + 1)
                    nc.gpsimd.tensor_tensor(hid[:, k % 4, 1, :], gated[:, k % 4, :], hid[:, k % 4, 0, :],
                                            ALU.subtract).then_inc(q["lo"], 1)
                    if k == STEPS0 + 5:
                        rstds(8 * i, G, 8 * i + 2 * TILES)
                rstds(8 * i + 4, G, 8 * i + (2 * TILES + 4))
            attention(1)

        @block.vector
        def _(dve):
            def carry_wait():
                nc.vector.tensor_copy(wait_carrier[:, 1:2], wait_carrier[:, 0:1])

            def spread(t, slot):
                nc.vector.bn_stats(stats[:, slot, :], x[:, t, :]).then_inc(s["st"], 1)

            def mean_var(slot):
                nc.vector.bn_aggr(mv_now[:, slot, :], stats[:, slot, :]).then_inc(s["agg"], 1)

            nc.vector.memset(col_raw[:, :], 0.0).then_inc(s["ones"], 1)
            nc.vector.memset(zero_eps[:, 0:1], 0.0)
            nc.vector.memset(wait_carrier[:, :], 0.0).then_inc(s["ones"], 1)
            nc.vector.memset(zero_eps[:, 1:2], EPS).then_inc(s["ones"], 1)
            nc.vector.memset(bias_rows[:, :, :], 0.0).then_inc(s["ones"], 1)
            nc.vector.memset(b2_rows[:, :], 0.0).then_inc(s["ones"], 1)
            nc.vector.memset(vals[:, :, :, :, :, :, :], 0.0).then_inc(s["ones"], 1)
            dve.wait_ge(s["ones"], 6)
            for h2 in range(2):
                r = slice(64 * h2, 64 * h2 + 64)
                nc.vector.memset(vals[r, :, 0, :, :, h2, HD:VW].rearrange("p t a b o -> p t (a b) o"), 1.0).then_inc(s["vone"], 1)
            dve.wait_ge(s["ids"], 16)
            nc.vector.tensor_copy(ident16[:, :], ident[:, :]).then_inc(s["cast16"], 1)
            for g in range(GROUPS):
                dve.wait_ge((s["ld_x0"], s["ld_x1"], s["ld_x2"], s["ld_x3"])[g], 16)
                positive_wait(dve, s["agg"], G * g)
                for t in range(G):
                    spread(G * g + t, t)
                dve.wait_ge(s["st"], G * g + G)
                positive_wait(dve, s["ag"], G * g)
                for t in range(G):
                    mean_var(t)
            for h in range(2):
                dve.wait_ge(s["wt_hi"], h + 1)
                nc.vector.scalar_tensor_tensor(wT[:, 1, 4 * h:4 * h + 4, :].rearrange("p a b -> p (a b)"), ps[:, h, :], WSCALE,
                                               wT[:, 0, 4 * h:4 * h + 4, :].rearrange("p a b -> p (a b)"),
                                               ALU.mult, ALU.subtract).then_inc(s["wt_lo"], 1)
            for g in range(GROUPS):
                dve.wait_ge(s["ct_hi"], g + 1)
                r = slice(g * GT, (g + 1) * GT)
                nc.vector.tensor_tensor(ctx_T[:, 1, r], ps[:, 2 + g, :], ctx_T[:, 0, r], ALU.subtract).then_inc(s["ct_lo"], 1)
            dve.wait_ge(s["wt_lo"], 2)
            dve.wait_ge(s["zero"], 1)
            for l in range(2):
                for i in range(2):
                    for j in range(QUAD):
                        c = slice(j * HD, (j + 1) * HD)
                        nc.vector.tensor_copy(wk_m[:, l, i, j, :].rearrange("p (g c) -> p g c", g=QUADS)[:, :, c],
                                              wT[:, i, 4 * l + 1, :].rearrange("p (g c) -> p g c", g=QUADS)[:, :, c]).then_inc(s["msk"], 1)
            dve.wait_ge(s["cst"], 64)
            dve.wait_ge(s["cols"], 1)
            for l in range(2):
                nc.vector.tensor_scalar(bk_m[:, l, :], quad_mask[:, :], bias_col[:, 2 * l + 1:2 * l + 2], None,
                                        ALU.mult).then_inc(s["bkm"], 1)
            for c in range(CHUNKS0):
                dve.wait_ge(s["ch_hi"], c + 1)
                nc.vector.scalar_tensor_tensor(w_out[c][:, 1, :], w_stage[:, c % 2, :], WSCALE, w_out[c][:, 0, :],
                                               ALU.mult, ALU.subtract).then_inc(s["ch_lo"], 1)
            dve.wait_ge(s["ld_s"], 16 * (8 + 2 + 3))
            nc.vector.tensor_scalar(bias_rows[0:1, :, :], bias_raw[0:1, :, :], WSCALE, None, ALU.mult).then_inc(s["small_hi"], 1)
            nc.vector.tensor_scalar(bias_hi[32:33, :, :], bias_raw[32:33, :, :], WSCALE, None, ALU.mult).then_inc(s["small_hi"], 1)
            for r in (HI_ROW, LO_ROW):
                nc.vector.tensor_scalar(b2_rows[r:r + EXPERTS, :], b2_raw[r:r + EXPERTS, :], WSCALE, None, ALU.mult).then_inc(s["small_hi"], 1)
            r = slice(HI2_ROW, HI2_ROW + EXPERTS)
            nc.vector.tensor_scalar(b2_hi[r, :], b2_raw[r, :], WSCALE, None, ALU.mult).then_inc(s["small_hi"], 1)
            for l in range(2):
                nc.vector.tensor_scalar(gate_w[:, l, 0, :], gate_raw[:, l, :], WSCALE, None, ALU.mult).then_inc(s["small_hi"], 1)
            dve.wait_ge(s["small_hi"], 7)
            nc.vector.scalar_tensor_tensor(bias_rows[32:33, :, :], bias_raw[32:33, :, :], WSCALE, bias_hi[32:33, :, :],
                                           ALU.mult, ALU.subtract).then_inc(s["small_lo"], 1)
            nc.vector.scalar_tensor_tensor(b2_rows[r, :], b2_raw[r, :], WSCALE, b2_hi[r, :], ALU.mult, ALU.subtract).then_inc(s["small_lo"], 1)
            for l in range(2):
                nc.vector.scalar_tensor_tensor(gate_w[:, l, 1, :], gate_raw[:, l, :], WSCALE, gate_w[:, l, 0, :],
                                               ALU.mult, ALU.subtract).then_inc(s["small_lo"], 1)

            def keys_values(l):
                q = KV[l]
                for g in range(GROUPS):
                    for j in range(QUAD):
                        n = QUAD * g + j
                        dve.wait_ge(q["k_hi"], n + 1)
                        hi, lo = (keys[:, G * g:G * (g + 1), c, :, j, :] for c in range(2))
                        f = k_f[:, n % 2, :].rearrange("p (t b k) -> p t b k", t=G, b=PER_TILE)
                        nc.vector.tensor_tensor(lo, f, hi, ALU.subtract).then_inc(q["k_lo"], 1)
                for j in range(TILES // 2):
                    dve.wait_ge(q["v_f"], j + 1)
                    if l == 1 and j == 0:
                        dve.wait_ge(A[0]["o_ps"], TILES)
                    parts = []
                    for h2 in range(2):
                        rows = slice(64 * h2, 64 * h2 + 64)
                        f = v_f[rows, j % 2, :].rearrange("p (s a h v) -> p s a h v", s=4, h=2, v=HD)
                        for i in range(2):
                            hi, lo = (vals[rows, 2 * j + i, c, :, :, h2, 0:HD].rearrange("p a b v -> p b a v") for c in range(2))
                            parts.append((hi, lo, f[:, 2 * i:2 * i + 2, :, h2, :]))
                    for n, (hi, lo, f) in enumerate(parts):
                        nc.vector.tensor_copy(hi, f).then_inc(s["vone"], 1)
                    dve.wait_ge(s["vone"], 2 + 4 * (j + 1) + 4 * (TILES // 2) * l)
                    for n, (hi, lo, f) in enumerate(parts):
                        nc.vector.tensor_tensor(lo, f, hi, ALU.subtract).then_inc(q["v_w"], 1)

            def attention(l):
                q = A[l]
                inv = 1 / WSCALE

                def step(t, u):
                    par = lambda k: (u + k) % 2 if not isinstance(t, int) else (t + k) % 2
                    if alive(t + 3):
                        hh = HEADS // 2
                        for h in range(2):
                            dve.wait_ge(q["s_ps"], 2 * t + (7 + h))
                            positive_wait(dve, q["sub"], 2 * t + (3 + h))
                            nc.vector.tensor_reduce(mx[:, par(3), h * hh:(h + 1) * hh], ps[:, h, :].rearrange("p (h k) -> p h k", k=SEQ),
                                                    axis=AX.X, op=ALU.max).then_inc(q["mx"], 1)
                    if alive(t + 6):
                        dve.wait_ge(s["rs"], t + (7 + 2 * l * TILES))
                        positive_wait(dve, q["xt_ps"], t + 5)
                        nc.vector.tensor_scalar(xhat[:, par(6), :], x[:, t + 6, :], mv[:, t + 6, 0:1],
                                                rstd[:, t + 6:t + 7] if isinstance(t, int) else rstd[:, bass.ds(t + 6, 1)],
                                                ALU.subtract, ALU.mult).then_inc(q["xh"], 1)
                    if alive(t + 3):
                        for h in range(2):
                            dve.wait_ge(q["mx"], 2 * t + (7 + h))
                            positive_wait(dve, q["p_ps"], 2 * t + (3 + h))
                            nc.vector.tensor_tensor(
                                probs[:, par(3), h * HALF:(h + 1) * HALF].rearrange("p (h k) -> p h k", k=SEQ),
                                ps[:, h, :].rearrange("p (h k) -> p h k", k=SEQ),
                                mx[:, par(3), h * hh:(h + 1) * hh].unsqueeze(2).broadcast_to([P, hh, SEQ]),
                                ALU.subtract).then_inc(q["sub"], 1)
                    if alive(t - 1):
                        dve.wait_ge(q["y_ps"], t)
                        at = t - 1 if isinstance(t, int) else bass.ds(t - 1, 1)
                        xt = x[:, at, :] if isinstance(t, int) else x[:, at, :].rearrange("p o d -> p (o d)")
                        nc.vector.scalar_tensor_tensor(xt, ps[:, 7, P:2 * P], inv, xt, ALU.mult, ALU.add).then_inc(q["res"], 1)
                    if alive(t + 5):
                        dve.wait_ge(q["xt_hi"], t + 6)
                        positive_wait(dve, q["q_ps"], t + 4)
                        nc.vector.tensor_tensor(xT[:, par(5), 1, :], ps[:, 4, 0:P], xT[:, par(5), 0, :],
                                                ALU.subtract).then_inc(q["xt_lo"], 1)
                    if alive(t - 1):
                        dve.wait_ge(q["res"], t)
                        dve.wait_ge(s["agg"], t + ((2 * l + 1) * TILES - 2))
                        carry_wait()
                        spread(t - 1, par(1))
                    if alive(t + 1):
                        dve.wait_ge(q["o_ps"], t + 2)
                        positive_wait(dve, q["ot_ps"], t)
                        o = ps[:, 5, 0:PAIRS * PER_TILE * 2 * VW].rearrange("p (a b h v) -> p a b h v", b=2, h=2, v=VW)
                        nc.vector.reciprocal(rden[:, par(1), :].rearrange("p (a h) -> p a h", h=2), o[:, :, 0, :, HD]).then_inc(q["rd"], 1)
                    if alive(t - 1):
                        dve.wait_ge(s["st"], t + (2 * l + 1) * TILES)
                        dve.wait_ge(s["ag"], t + ((2 * l + 1) * TILES - 2))
                        carry_wait()
                        mean_var(par(1))
                    if alive(t + 1):
                        dve.wait_ge(q["rd"], t + 2)
                        for b in range(PER_TILE):
                            rows = slice(64 * b, 64 * b + 64)
                            nc.vector.tensor_tensor(
                                o_n[rows, par(1), :].rearrange("p (a h v) -> p a h v", h=2, v=HD), o[rows, :, b, :, 0:HD],
                                rden[rows, par(1), :].rearrange("p (a h o) -> p a h o", h=2, o=1).broadcast_to([64, PAIRS, 2, HD]),
                                ALU.mult).then_inc(q["on"], 1)
                    if alive(t):
                        dve.wait_ge(q["ot_hi"], t + 1)
                        positive_wait(dve, q["y_ps"], t - 1)
                        nc.vector.tensor_tensor(oT[:, par(0), 1, :], ps[:, 6, 0:P], oT[:, par(0), 0, :],
                                                ALU.subtract).then_inc(q["ot_lo"], 1)
                    if alive(t + 2):
                        positive_wait(dve, q["o_ps"], t + 1)
                        dve.wait_ge(q["p_hi"], 2 * t + 5)
                        nc.vector.tensor_tensor(pT[:, par(2), 1, 0:4, :].rearrange("p a b -> p (a b)"), ps[:, 2, :],
                                                pT[:, par(2), 0, 0:4, :].rearrange("p a b -> p (a b)"), ALU.subtract).then_inc(q["p_lo"], 1)

                pipeline(dve, step, TILES, 6)

            def routing(l):
                q = F[l]
                nc.vector.memset(comb16[:, :, :], 0.0).then_inc(q["c16"], 1)
                for g in range(GROUPS):
                    if g >= 2:
                        dve.wait_ge(q["xt_ps"], g - 1)
                    for t in range(G * g, G * g + G):
                        dve.wait_ge(s["rs"], t + (1 + (2 * l + 1) * TILES))
                        nc.vector.tensor_scalar(fx[:, g % 2, (t % G) * P:(t % G + 1) * P], x[:, t, :], mv[:, t, 0:1], rstd[:, t:t + 1],
                                                ALU.subtract, ALU.mult).then_inc(q["xh"], 1)
                    if g >= 1:
                        low(q, g - 1)
                low(q, GROUPS - 1)
                dve.wait_ge(q["lg_ps"], 1)
                nc.vector.tensor_scalar(logits, ps[:, 4, 0:TILES * EXPERTS].rearrange("p (t e) -> p t e", e=EXPERTS),
                                        1 / WSCALE, None, ALU.mult).then_inc(q["lg"], 1)
                dve.wait_ge(q["lg"], 1)
                for t in range(TILES):
                    nc.vector.max(top_v[:, t, :], logits[:, t, :]).then_inc(q["top"], 1)
                for t in range(TILES):
                    dve.wait_ge(q["top"], t + 1)
                    nc.vector.max_index(top_i[:, t, :], top_v[:, t, :], logits[:, t, :]).then_inc(q["idx"], 1)
                nc.vector.tensor_tensor(diff, top_v[:, :, 1], top_v[:, :, 0], ALU.subtract).then_inc(q["dif"], 1)
                dve.wait_ge(q["idx"], TILES)
                nc.vector.tensor_copy(top_f, top_i[:, :, 0:2]).then_inc(q["idx"], 1)
                dve.wait_ge(q["idx"], TILES + 1)
                dve.wait_ge(s["cst"], 64)
                for c in range(2):
                    nc.vector.tensor_tensor(one_hot[:, c, :, :], iota8[:, :].unsqueeze(1).broadcast_to([P, TILES, EXPERTS]),
                                            top_f[:, :, c:c + 1].broadcast_to([P, TILES, EXPERTS]), ALU.is_equal).then_inc(q["oh"], 1)
                dve.wait_ge(q["ex"], 1)
                nc.vector.tensor_scalar(diff, prob[:, :, 1], 1.0, None, ALU.add).then_inc(q["pr"], 1)
                dve.wait_ge(q["pr"], 1)
                nc.vector.reciprocal(prob[:, :, 0], diff).then_inc(q["pr"], 1)
                dve.wait_ge(q["pr"], 2)
                nc.vector.tensor_tensor(prob[:, :, 1], prob[:, :, 1], prob[:, :, 0], ALU.mult).then_inc(q["pr"], 1)
                dve.wait_ge(q["pr"], 3)
                dve.wait_ge(q["oh"], 2)
                for c in range(2):
                    nc.vector.tensor_tensor(one_hot[:, c, :, :], one_hot[:, c, :, :],
                                            prob[:, :, c:c + 1].broadcast_to([P, TILES, EXPERTS]), ALU.mult).then_inc(q["oh"], 1)
                dve.wait_ge(q["oh"], 4)
                nc.vector.tensor_tensor(comb, one_hot[:, 0, :, :], one_hot[:, 1, :, :], ALU.add).then_inc(q["cb"], 1)
                dve.wait_ge(q["cb"], 1)
                dve.wait_ge(q["c16"], 1)
                for col in (HI_ROW, HI2_ROW):
                    nc.vector.tensor_copy(comb16[:, :, col:col + EXPERTS], comb).then_inc(q["c16"], 1)
                dve.wait_ge(q["c16"], 3)
                nc.vector.tensor_tensor(comb16[:, :, LO_ROW:LO_ROW + EXPERTS], comb, comb16[:, :, HI_ROW:HI_ROW + EXPERTS],
                                        ALU.subtract).then_inc(q["c16"], 1)
                dve.wait_ge(q["ct_ps"], 1)
                nc.vector.tensor_copy(combT[:, tokens // 2:tokens], half_bank[3]).then_inc(q["ct_lo"], 1)

            def low(q, g):
                dve.wait_ge(q["xt_hi"], g + 1)
                r = slice(g * GT, (g + 1) * GT)
                nc.vector.tensor_tensor(xTa[:, 1, r], ps[:, g % 2, :], xTa[:, 0, r], ALU.subtract).then_inc(q["xt_lo"], 1)

            def experts0():
                q = F[0]
                with dve.Fori(0, GROUPS // 2) as i:
                    for k in range(2 * STEPS0):
                        n = 2 * STEPS0 * i + k
                        dve.wait_ge(q["act"], n + 1)
                        nc.vector.scalar_tensor_tensor(act_f[:, k % 4, :], ps[:, 2 + k % 2, :], 1 / WSCALE, act_f[:, k % 4, :],
                                                       ALU.mult, ALU.mult).then_inc(q["t1"], 1)
                        dve.wait_ge(q["t1"], n + 1)
                        if k >= 4:
                            dve.wait_ge(q["lo"], n - 3)
                        nc.vector.tensor_tensor(gated[:, k % 4, :], ps[:, 4 + k % 2, :], act_f[:, k % 4, :], ALU.mult).then_inc(q["gt"], 1)
                        if k in CHUNK_STEPS:
                            m = CHUNK_STEPS.index(k)
                            dve.wait_ge(s["ch_hi"], 4 * i + (CHUNKS0 + m + 1))
                            nc.vector.scalar_tensor_tensor(w12[:, 1, 4 * i + m, :], w_stage[:, (CHUNKS0 + m) % 2, 0:CHUNK1], WSCALE,
                                                           w12[:, 0, 4 * i + m, :], ALU.mult, ALU.subtract).then_inc(s["ch_lo"], 1)
                        if k == STEPS0 + 4:
                            residual0(i, 0)
                    residual0(i, 1)

            def residual0(i, half):
                q = F[0]
                gi = 2 * i + half
                dve.wait_ge(q["down"], 2 * STEPS0 * i + STEPS0 * (half + 1))
                nc.vector.scalar_tensor_tensor(
                    x[:, bass.ds(8 * i + 4 * half, G), :].rearrange("p t d -> p (t d)"), ps[:, 6 + half, :], 1 / WSCALE,
                    x[:, bass.ds(8 * i + 4 * half, G), :].rearrange("p t d -> p (t d)"), ALU.mult, ALU.add).then_inc(q["res"], 1)
                n = 2 * TILES + 8 * i + 4 * half
                dve.wait_ge(q["res"], gi + 1)
                dve.wait_ge(s["agg"], n)
                carry_wait()
                for t in range(G):
                    spread(8 * i + (4 * half + t), t)
                dve.wait_ge(s["st"], n + G)
                dve.wait_ge(s["ag"], n)
                carry_wait()
                for t in range(G):
                    mean_var(t)

            def experts1():
                q = F[1]
                for g in range(GROUPS):
                    dve.wait_ge(q["b2_ps"], g + 1)
                    r = x[:, G * g:G * (g + 1), :].rearrange("p t d -> p (t d)")
                    nc.vector.scalar_tensor_tensor(r, ps[:, 4 + g % 2, :], 1 / WSCALE, r, ALU.mult, ALU.add).then_inc(q["b2_r"], 1)
                dve.wait_ge(q["c16"], 4)
                nc.vector.tensor_scalar(comb, comb, 1 / WSCALE, None, ALU.mult).then_inc(q["cb"], 1)
                dve.wait_ge(q["cb"], 2)
                dve.wait_ge(q["b2_r"], GROUPS)
                K = GROUPS * STEPS1

                def expert(e):
                    for k in range(K):
                        n = K * e + k
                        dve.wait_ge(q["hi"], n + 1)
                        positive_wait(dve, q["down"], n - 3)
                        nc.vector.tensor_tensor(hid[:, k % 4, 1, :], act_f[:, k % 4, :], hid[:, k % 4, 0, :], ALU.subtract).then_inc(q["lo"], 1)
                        if k % STEPS1 == 2:
                            if k > STEPS1:
                                accumulate(e, k // STEPS1 - 1, GROUPS * e + k // STEPS1)
                            elif not isinstance(e, int):
                                accumulate(e - 1, GROUPS - 1, GROUPS * e)

                expert(0)
                with dve.Fori(1, EXPERTS) as e:
                    expert(e)
                accumulate(EXPERTS - 1, GROUPS - 1, GROUPS * EXPERTS)

            def accumulate(e, g, done):
                q = F[1]
                dve.wait_ge(q["down"], STEPS1 * done)
                for t in range(G):
                    ins = nc.vector.scalar_tensor_tensor(x[:, G * g + t, :], ps[:, 4 + g % 2, t * P:(t + 1) * P],
                                                         comb[:, G * g + t, bass.ds(e, 1)], x[:, G * g + t, :], ALU.mult, ALU.add)
                ins.then_inc(q["res"], 1)

            keys_values(0)
            attention(0)
            routing(0)
            experts0()
            keys_values(1)
            attention(1)
            routing(1)
            experts1()

        @block.tensor
        def _(pe):
            def three(dst, lhs, rhs, start=True, stop=True, **kw):
                pe.matmul(dst, lhs[0], rhs[0], start=start, stop=False, **kw)
                pe.matmul(dst, lhs[0], rhs[1], start=False, stop=False, **kw)
                return pe.matmul(dst, lhs[1], rhs[0], start=False, stop=stop, **kw)

            pe.wait_ge(s["ids"], 16)
            pe.wait_ge(s["ld_w"], 16 * 8)
            for h in range(2):
                for n in range(4):
                    mm = pe.transpose(ps[:, h, n * P:(n + 1) * P], w_raw[:, 4 * h + n, :], ident[:, :])
                mm.then_inc(s["wt_ps"], 1)
            pe.wait_ge(s["ld_k"], 16 * 5)
            pe.transpose(ps[:, 6, 0:P], col_raw[:, :], ident[:, :]).then_inc(s["col_ps"], 1)
            pe.wait_ge(s["ld_c"], 16 * GROUPS)
            for g in range(GROUPS):
                for n in range(G):
                    mm = pe.transpose(ps[:, 2 + g, n * P:(n + 1) * P], ctx_raw[:, G * g + n, :], ident[:, :])
                mm.then_inc(s["ct_ps"], 1)
            pe.wait_ge(s["wt_lo"], 2)
            pe.wait_ge(s["ct_lo"], GROUPS)
            pe.wait_ge(s["small_lo"], 1)
            pe.wait_ge(s["msk"], 4 * QUAD)
            pe.wait_ge(s["cst"], 64)

            def W(l, which):
                n = 4 * l + "qkvo".index(which)
                return wT[:, 0, n, :], wT[:, 1, n, :]

            def keys_values(l):
                q = KV[l]
                for g in range(GROUPS):
                    r = slice(g * GT, (g + 1) * GT)
                    for j in range(QUAD):
                        n = QUAD * g + j
                        if n >= 2:
                            pe.wait_ge(q["k_f"], n - 1)
                        three(ps[:, n % 2, :], (wk_m[:, l, 0, j, :], wk_m[:, l, 1, j, :]),
                              (ctx_T[:, 0, r], ctx_T[:, 1, r])).then_inc(q["k_ps"], 1)
                wv = W(l, "v")
                for j in range(TILES // 2):
                    if j >= 2:
                        pe.wait_ge(q["v_f"], j - 1)
                    for n in range(4):
                        c = [ctx_T[:, i, (4 * j + n) * SEQ:(4 * j + n + 1) * SEQ] for i in range(2)]
                        cols_n = slice(n * P, (n + 1) * P)
                        pe.matmul(ps[:, 4 + j % 2, cols_n], two_rows[:, :], bias_rows[:, 2 * l, :], start=True, stop=False)
                        for ci, wi in ((0, 0), (0, 1), (1, 0)):
                            for h2 in range(2):
                                mm = pe.matmul(ps[64 * h2:64 * h2 + 64, 4 + j % 2, cols_n], c[ci], wv[wi], start=False, stop=(ci == 1))
                    mm.then_inc(q["v_ps"], 1)

            def attention(l):
                q = A[l]
                pe.wait_ge(KV[l]["v_w"], 4 * (TILES // 2))

                def step(t, u):
                    par = lambda k: (u + k) % 2 if not isinstance(t, int) else (t + k) % 2
                    if alive(t + 4):
                        pe.wait_ge(q["xt_lo"], t + 5)
                        positive_wait(pe, q["q_act"], 5 * t + 20)
                        positive_wait(pe, q["res"], t - 1)
                        three(ps[:, 7, 0:P], W(l, "q"), (xT[:, par(4), 0, :], xT[:, par(4), 1, :])).then_inc(q["q_ps"], 1)
                    if alive(t + 5):
                        pe.wait_ge(q["xh"], t + 6)
                        positive_wait(pe, q["xt_lo"], t + 5)
                        pe.transpose(ps[:, 4, 0:P], xhat[:, par(5), :], ident[:, :]).then_inc(q["xt_ps"], 1)
                    if alive(t + 3):
                        pr = par(3)
                        pe.wait_ge(q["q_lo"], QUADS * t + 4 * QUADS)
                        if isinstance(t, int):
                            pe.wait_ge((q["kb0"], q["kb1"])[pr], 16 * ((t + 3) // 2 + 1))
                        else:
                            pe.wait_ge((q["kb0"], q["kb1"])[pr], 8 * t + (32 + 8 * u))
                        for n in range(QUADS):
                            if n % 2 == 0:
                                positive_wait(pe, q["sub"], 2 * t + (5 + n // 2))
                            for qi, ki in ((0, 0), (0, 1), (1, 0)):
                                for b in range(PER_TILE):
                                    c = QUAD * SEQ * (n % 2)
                                    mm = pe.matmul(ps[64 * b:64 * b + 64, n // 2, c:c + QUAD * SEQ], q_blk[:, pr, qi, n, 64 * b:64 * b + 64],
                                                   keys_now[:, pr, ki, b, :], start=(qi + ki == 0), stop=(qi == 1))
                            if n % 2 == 1:
                                mm.then_inc(q["s_ps"], 1)
                    if alive(t - 1):
                        pe.wait_ge(q["ot_lo"], t)
                        positive_wait(pe, q["res"], t - 1)
                        pe.wait_ge(q["q_act"], 5 * within(t + 5))
                        dst = ps[:, 7, P:2 * P]
                        three(dst, (oT[:, par(1), 0, :], oT[:, par(1), 1, :]), W(l, "o"), stop=False)
                        pe.matmul(dst, two_rows[:, :], bias_rows[:, 2 * l + 1, :], start=False, stop=True).then_inc(q["y_ps"], 1)
                    if alive(t + 1):
                        positive_wait(pe, q["on"], 2 * t + 2)
                        pe.wait_ge(q["p_lo"], t + 2)
                        pr = par(1)
                        pe.wait_ge((q["vb0"], q["vb1"])[pr], 16 * ((t + 1) // 2 + 1) if isinstance(t, int) else 8 * t + (16 + 8 * u))
                        pe.wait_ge(q["p_lop"], t + 2)
                        for n in range(PAIRS):
                            w = PER_TILE * 2 * VW
                            v = [vals_now[:, pr, i, n, :] for i in range(2)]
                            mm = three(ps[:, 5, n * w:(n + 1) * w], (pT[:, par(1), 0, n, :], pT[:, par(1), 1, n, :]), v)
                        mm.then_inc(q["o_ps"], 1)
                    if alive(t):
                        pe.wait_ge(q["on"], 2 * t + 2)
                        positive_wait(pe, q["ot_lo"], t)
                        pe.transpose(ps[:, 6, 0:P], o_n[:, par(0), :], ident[:, :]).then_inc(q["ot_ps"], 1)
                    if alive(t + 2):
                        for h in range(2):
                            pe.wait_ge(q["ex"], 2 * t + (5 + h))
                            positive_wait(pe, (q["p_lo"], q["p_f"])[h], t + 2)
                            for n in range(4):
                                c = (4 * h + n) * P
                                mm = pe.transpose(ps[:, 2 + h, n * P:(n + 1) * P], probs[:, par(2), c:c + P], ident[:, :])
                            mm.then_inc(q["p_ps"], 1)

                pipeline(pe, step, TILES, 6)

            def routing(l):
                q = F[l]
                pe.wait_ge(A[l]["res"], TILES)
                pe.wait_ge(s["small_lo"], 4)
                for g in range(GROUPS):
                    if g >= 2:
                        pe.wait_ge(q["xt_lo"], g - 1)
                    for n in range(G):
                        pe.wait_ge(q["xh"], G * g + n + 1)
                        mm = pe.transpose(ps[:, g % 2, n * P:(n + 1) * P], fx[:, g % 2, n * P:(n + 1) * P], ident[:, :])
                    mm.then_inc(q["xt_ps"], 1)
                for t in range(TILES):
                    pe.wait_ge(q["xt_lo"], t // G + 1)
                    r = slice(t * P, (t + 1) * P)
                    mm = three(ps[:, 4, t * EXPERTS:(t + 1) * EXPERTS], (xTa[:, 0, r], xTa[:, 1, r]),
                               (gate_w[:, l, 0, :], gate_w[:, l, 1, :]))
                mm.then_inc(q["lg_ps"], 1)
                pe.wait_ge(q["c16"], 4)
                for t in range(TILES):
                    c = (t % 8) * P
                    mm = pe.transpose(half_bank[2 + t // 8][:, c:c + P], comb16[:, t, :], ident16[:, :])
                mm.then_inc(q["ct_ps"], 1)
                pe.wait_ge(q["ct_hi"], 1)
                pe.wait_ge(q["ct_lo"], 1)

            def down(dst, h, w, first, last):
                for t in range(G):
                    r = slice(t * P, (t + 1) * P)
                    mm = three(dst[:, r], (h[:, 0, r], h[:, 1, r]), w, start=first and t == 0, stop=last, skip_group_check=True)
                return mm

            def experts0():
                q = F[0]
                pe.wait_ge(s["ch_lo"], CHUNKS0)
                K = 2 * STEPS0
                LAG = 3
                with pe.Fori(0, GROUPS // 2) as i:
                    for k in range(K + LAG):
                        if k < K:
                            n = K * i + k
                            f = slice((k % STEPS0) * P, (k % STEPS0 + 1) * P)
                            tok = bass.ds(1024 * i + GT * (k // STEPS0), GT)
                            xs = (xTa[:, 0, tok], xTa[:, 1, tok])
                            if k >= 2:
                                pe.wait_ge(q["gt"], n - 1)
                            three(ps[:, k % 2, :], (wg[:, 0, f], wg[:, 1, f]), xs)
                            three(ps[:, 2 + k % 2, :], (wu[:, 0, f], wu[:, 1, f]), xs)
                            pe.matmul(ps[:, 4 + k % 2, :], expert_rows[:, f], combT[:, tok], start=True, stop=True).then_inc(q["up"], 1)
                        if k >= LAG:
                            j = k - LAG
                            pe.wait_ge(q["lo"], K * i + (j + 1))
                            half, f = divmod(j, STEPS0)
                            down(ps[:, 6 + half, :], hid[:, j % 4, :, :],
                                 (wd[:, 0, f * P:(f + 1) * P], wd[:, 1, f * P:(f + 1) * P]), f == 0, f == STEPS0 - 1).then_inc(q["down"], 1)
                    pe.wait_ge(q["res"], 2 * i + 2)

            def experts1():
                q = F[1]
                pe.wait_ge(s["small_lo"], 4)
                for g in range(GROUPS):
                    if g >= 2:
                        pe.wait_ge(q["b2_r"], g - 1)
                    for t in range(G):
                        r = slice((G * g + t) * P, (G * g + t + 1) * P)
                        mm = pe.matmul(ps[:, 4 + g % 2, t * P:(t + 1) * P], combT[:, r], b2_rows[:, :], start=True, stop=True)
                    mm.then_inc(q["b2_ps"], 1)
                pe.wait_ge(q["b2_r"], GROUPS)
                pe.wait_ge(s["ch_lo"], len(chunks))
                K = GROUPS * STEPS1
                LAG = 3

                def up(e, k, n):
                    g, f = divmod(k, STEPS1)
                    fs = slice(f * P, (f + 1) * P)
                    r = slice(g * GT, (g + 1) * GT)
                    positive_wait(pe, q["act"], n - 3)
                    three(ps[:, k % 4, :], (w1[:, 0, e, fs], w1[:, 1, e, fs]),
                          (xTa[:, 0, r], xTa[:, 1, r])).then_inc(q["up"], 1)

                def expert(e, ahead):
                    for k in range(K):
                        if k + LAG < K:
                            up(e, k + LAG, K * e + (k + LAG))
                        elif ahead:
                            up(e + 1, k + LAG - K, K * e + (k + LAG))
                        g, f = divmod(k, STEPS1)
                        pe.wait_ge(q["lo"], K * e + (k + 1))
                        if f == 0:
                            positive_wait(pe, q["res"], GROUPS * e + (g - 1))
                        down(ps[:, 4 + g % 2, :], hid[:, k % 4, :, :], (w2[:, 0, e, f, :], w2[:, 1, e, f, :]),
                             f == 0, f == STEPS1 - 1).then_inc(q["down"], 1)

                for k in range(LAG):
                    up(0, k, k)
                expert(0, True)
                with pe.Fori(1, EXPERTS - 1) as e:
                    expert(e, True)
                expert(EXPERTS - 1, False)

            keys_values(0)
            attention(0)
            routing(0)
            experts0()
            pe.wait_ge(F[0]["res"], GROUPS)
            keys_values(1)
            attention(1)
            routing(1)
            experts1()


def constants():
    rows = np.zeros((P, HID0), np.float16)
    for r in (HI_ROW, LO_ROW):
        rows[r + np.arange(HID0) // M0, np.arange(HID0)] = 1
    two = np.zeros((P, P), np.float16)
    two[[0, 32]] = 1
    quad = np.arange(P)[:, None] % 32 // HD == np.arange(QUAD)[None, :]
    return {"quad_mask": quad.astype(np.float32), "ident": np.eye(P, dtype=np.float32), "expert_rows": rows, "two_rows": two,
            "iota8": np.broadcast_to(np.arange(EXPERTS, dtype=np.float32), (P, EXPERTS)).copy()}


def kernel(**inputs):
    import concourse.bacc as bacc
    from concourse.bass_utils import run_bass_kernel_spmd

    nc = bacc.Bacc("TRN2", target_bir_lowering=False, num_devices=1)
    arrays, args = {}, {}
    for name, value in {**inputs, **constants()}.items():
        v = np.ascontiguousarray(value)
        arrays[f"in_{name}"] = v
        args[name] = nc.dram_tensor(f"in_{name}", v.shape, mybir.dt.from_np(v.dtype), kind="ExternalInput").ap()
    out = nc.dram_tensor("out", inputs["x"].shape, F32, kind="ExternalOutput").ap()
    build(nc, args, out)
    r = run_bass_kernel_spmd(nc, [arrays], core_ids=[0])
    return r.results[0]["out"]
```

```python
from contextlib import ExitStack

import numpy as np

import concourse.bass as bass
from concourse import mybir

F32 = mybir.dt.float32
F16 = mybir.dt.float16
U32 = mybir.dt.uint32
ALU = mybir.AluOpType
ACT = mybir.ActivationFunctionType
AX = mybir.AxisListType

P = 128
SEQ = 64
PER_TILE = P // SEQ
D = 128
HEADS = 16
HD = D // HEADS
PAIRS = HEADS // 2
QUADS = 4
QUAD = HEADS // QUADS
HALF = HEADS * SEQ // 2
VW = HD + 1
EXPERTS = 8
M0 = 176
M1 = 512
HID0 = EXPERTS * M0
STEPS0 = HID0 // P
STEPS1 = M1 // P
G = 4
EPS = 1e-5
WSCALE = 1024.0
HI_ROW, LO_ROW, HI2_ROW = 0, 32, 64


def positive_wait(eng, sem, value):
    if not isinstance(value, int) or value > 0:
        eng.wait_ge(sem, value)


def pipeline(eng, step, tiles, ahead, between):
    first = 2
    last = (tiles - ahead - first) // 2 * 2 + first
    for t in range(-ahead, first):
        step(t, 0)
        if t + ahead < 3:
            between(t + ahead)
    with eng.Fori(0, (last - first) // 2) as i:
        step(2 * i + first, 0)
        step(2 * i + (first + 1), 1)
    for t in range(last, tiles + 1):
        step(t, 0)


def build(nc, a, out):
    tokens = a["x"].shape[0] * a["x"].shape[1]
    TILES = tokens // P
    GROUPS = TILES // G
    GT = G * P

    with ExitStack() as ctx:
        def sb(name, shape, dt):
            return ctx.enter_context(nc.sbuf_tensor(name, shape, dt))

        def sems(names, suffix=""):
            return {n: ctx.enter_context(nc.semaphore(n + suffix)) for n in names.split()}

        x = sb("x_res", [P, TILES, D], F32)
        mv = sb("mean_var", [P, TILES, 2], F32)
        rstd = sb("rstd", [P, TILES], F32)
        mv_now = sb("mv_now", [P, G, 2], F32)
        act_warm = sb("act_warm", [P, 2], F32)
        zero_eps = sb("zero_eps", [P, 2], F32)
        b1_now = sb("b1_now", [P, STEPS1], F32)
        minus_half = sb("minus_half", [P, 1], F32)
        stats = sb("stats", [P, G, 6], F32)
        wait_carrier = sb("wait_carrier", [P, 2], F32)
        ident = sb("ident", [P, P], F32)
        ident16 = sb("ident16", [P, P], F16)
        iota8 = sb("iota8", [P, EXPERTS], F32)
        expert_rows = sb("expert_rows", [P, HID0], F16)
        two_rows = sb("two_rows", [P, P], F16)
        w_raw = sb("w_raw", [P, 8, P], F32)
        wT = sb("wT", [P, 2, 8, P], F16)
        col_raw = sb("col_raw", [P, P], F32)
        cols = sb("cols", [P, P], F32)
        N_B1 = EXPERTS * STEPS1
        bias_col = cols[:, N_B1:N_B1 + 4]
        b1_col = cols[:, 0:N_B1].rearrange("p (e j) -> p e j", j=STEPS1)
        bias_raw = sb("bias_raw", [33, 4, P], F32)
        bias_hi = sb("bias_hi", [33, 4, P], F16)
        bias_rows = sb("bias_rows", [P, 4, P], F16)
        gate_raw = sb("gate_raw", [P, 2, EXPERTS], F32)
        gate_w = sb("gate_w", [P, 2, 2, EXPERTS], F16)
        b2_raw = sb("b2_raw", [P, D], F32)
        b2_hi = sb("b2_hi", [P, D], F16)
        b2_rows = sb("b2_rows", [P, D], F16)
        ctx_T = sb("ctx_T", [P, 2, tokens], F16)
        keys = sb("keys", [P, TILES, 2, PER_TILE, QUAD, SEQ], F16)
        keys_now = sb("keys_now", [P, 2, 2, PER_TILE, QUAD * SEQ], F16)
        q_f = sb("q_f", [P, 2, QUADS, P], F32)
        q_blk = sb("q_blk", [P, 2, 2, QUADS, P], F16)
        wk_m = sb("wk_m", [P, 2, 2, QUAD, P], F16)
        quad_mask = sb("quad_mask", [P, QUAD], F32)
        bk_m = sb("bk_m", [P, 2, QUAD], F32)
        vals_flat = sb("vals", [P, 2 * TILES * PER_TILE * PAIRS * 2 * VW], F16)
        vals = vals_flat[:, :].rearrange("p (i t b a h v) -> p i t b a h v", i=2, t=TILES, b=PER_TILE, a=PAIRS, h=2)
        vals_now = sb("vals_now", [P, 2, 2, PER_TILE, PAIRS, 2 * VW], F16)
        wg = sb("wg", [P, 2, HID0], F16)
        wu = sb("wu", [P, 2, HID0], F16)
        wd = sb("wd", [P, 2, HID0], F16)
        w12_flat = sb("w12", [P, 2 * 2 * EXPERTS * M1], F16)
        w12 = w12_flat[:, :].rearrange("p (i c n) -> p i c n", i=2, c=8)
        w1 = w12[:, :, 0:4, :].rearrange("p i c (e f) -> p i (c e) f", f=M1)
        w2 = w12[:, :, 4:8, :].rearrange("p i c (e j d) -> p i (c e) j d", j=STEPS1, d=D)
        w_stage = sb("w_stage", [P, 2, 2 * M1], F32)
        w_stage0 = [w12_flat[:, :].bitcast(F32)[:, n * HID0:(n + 1) * HID0] for n in range(3)]
        area = sb("area", [P, 12400], F32)
        used = [0]

        def carve(shape, dt):
            n = int(np.prod(shape)) * (2 if dt == F16 else 4) // 4
            ap = area[:, used[0]:used[0] + n]
            used[0] += n
            assert used[0] <= 12400, used
            if dt == F16:
                ap = ap.bitcast(F16)
            names = "abcd"[:len(shape)]
            if len(shape) > 1:
                ap = ap.rearrange(f"p ({' '.join(names)}) -> p {' '.join(names)}", **dict(zip(names[1:], shape[1:])))
            return ap

        xhat = carve([2, P], F32)
        xT = carve([2, 2, P], F16)
        xT_f = carve([2, P], F32)
        mx = carve([2, HEADS], F32)
        probs = carve([2, HEADS * SEQ], F32)
        pT = carve([2, 2, PAIRS, P], F16)
        p_f = carve([2, 4 * P], F32)
        rden = carve([2, HEADS], F32)
        o_n = carve([2, P], F32)
        oT = carve([2, 2, P], F16)
        used[0] = 0
        ctx_raw = carve([TILES, D], F32)
        k_f = carve([4, GT], F32)
        v_f = carve([2, GT], F32)
        used[0] = 0
        act_f = carve([4, GT], F32)
        gated = carve([4, GT], F32)
        hid = carve([4, 2, GT], F16)
        combT = carve([tokens], F16)
        fx = carve([2, G * P], F32)
        xTa = carve([2, tokens], F16)
        logits = carve([TILES, EXPERTS], F32)
        top_v = carve([TILES, 8], F32)
        top_i = carve([TILES, 8], F32).bitcast(U32)
        top_f = carve([TILES, 2], F32)
        diff = carve([TILES], F32)
        prob = carve([TILES, 2], F32)
        one_hot = carve([2, TILES, EXPERTS], F32)
        comb = carve([TILES, EXPERTS], F32)
        comb16 = carve([TILES, P], F16)

        ps = ctx.enter_context(nc.psum_tensor("ps", [P, 8, 512], F32))
        half_bank = [ps[:, b, :].bitcast(F16) for b in range(8)]
        xta_bank = (4, 0, 1, 4)
        logit_bank = (3, 5)
        NORMALISE, TRANSPOSE, HIGH, LOW, LOGITS, RANK = (10, 12, 13), (11, 13, 14), (12, 14, 15), (13, 14, 15), (14, 15, 16), (15, 16)

        s = sems("ld_x0 ld_x1 ld_x2 ld_x3 ld_c ld_w0 ld_w1 ld_k ld_s col_ps cols ids ones wt_ps wt_hi wt_lo ct_ps ct_hi ct_lo small_hi small_lo "
                 "zero st agg ag rs out_d "
                 "ch0_in ch_in0 ch_in1 ch_hi ch_lo cst msk bkm")
        KV = [sems("k_ps k_f k_hi k_dve pool v_ps v_f v_w", f"_kv{l}") for l in range(2)]
        A = [sems("vb0 vb1 p_f p_lop kb0 kb1 xh xt_ps xt_hi xt_lo q_ps q_act q_lo s_ps mx sub ex p_ps p_hi p_lo o_ps rd on "
                  "ot_ps ot_hi ot_lo y_ps res", f"_a{l}") for l in range(2)]
        F = [sems("xh xt_ps xt_hi xt_lo lg_ps lg top idx ex pr oh cb c16 ct_ps ct_a ct_d "
                  "up act hi lo down res " + ("t1 gt", "b1 b2_ps b2_r")[l], f"_f{l}") for l in range(2)]

        w_in = [a["L0_ffn_w_g"].rearrange("e d m -> d e m"), a["L0_ffn_w_u"].rearrange("e d m -> d e m"),
                a["L0_ffn_w_d"].rearrange("e m d -> (e m) d").rearrange("(j p) d -> p j d", p=P)]
        w_out = [wg, wu, wd]
        chunks = [a["L1_ffn_W1"][e:e + 2].rearrange("e d f -> d e f") for e in range(0, EXPERTS, 2)]
        chunks += [a["L1_ffn_W2"][e:e + 2].rearrange("e (j p) d -> p (e j) d", p=P) for e in range(0, EXPERTS, 2)]
        CHUNK_STEPS = (2, 7, 12, 17)
        x_dram = a["x"].rearrange("b s d -> (b s) d").rearrange("(t p) d -> p t d", p=P)
        c_dram = a["ctx_1024"].rearrange("b s d -> (b s) d").rearrange("(t p) d -> p t d", p=P)
        out_dram = out.rearrange("b s d -> (b s) d").rearrange("(t p) d -> p t d", p=P)
        W_NAMES = [f"L{l}_xattn_W{n}" for l in range(2) for n in "qkvo"]

        def alive(t):
            return not isinstance(t, int) or 0 <= t < TILES

        WT_BANK = (0, 6)
        VALUE_PARTS = (range(0, 3), range(3, 5), range(5, TILES // 2))
        LAYER0_SPLITS = (1, 3, 5)

        def wait_keys_split(eng, l, n):
            if n % 2 == 0:
                eng.wait_ge(KV[l]["pool"], n // 2 + 1)
            else:
                eng.wait_ge(KV[l]["k_dve"], n + 1)

        def value_parts(j, h2):
            rows = slice(64 * h2, 64 * h2 + 64)
            f = v_f[rows, j % 2, :].rearrange("p (s a h v) -> p s a h v", s=4, h=2, v=HD)[:, :, :, h2, :]
            hi, lo = (vals[rows, c, 2 * j:2 * j + 2, :, :, h2, 0:HD].rearrange("p t b a v -> p (t b) a v") for c in range(2))
            return hi, lo, f

        def wait_values_split(eng, l, j):
            eng.wait_ge(KV[l]["v_w"], 3 * (j + 1))
            eng.wait_ge(KV[l]["pool"], GROUPS * QUAD // 2 + j + 1)

        def within(count):
            return min(count, TILES) if isinstance(count, int) else count

        block = ctx.enter_context(nc.Block())

        @block.sync
        def _(sp):
            sp.dma_start(ident[:, :], a["ident"]).then_inc(s["ids"], 16)

            def load_weights(l):
                for n in range(4 * l, 4 * l + 4):
                    sp.dma_start(w_raw[:, n, :], a[W_NAMES[n]]).then_inc((s["ld_w0"], s["ld_w1"])[l], 16)

            load_weights(0)
            for g in range(GROUPS):
                sp.dma_start(ctx_raw[:, G * g:G * (g + 1), :], c_dram[:, G * g:G * (g + 1), :]).then_inc(s["ld_c"], 16)
            sp.wait_ge(s["ones"], 1)
            sp.dma_start(two_rows[:, :], a["two_rows"]).then_inc(s["ld_s"], 16)
            for n, name in enumerate(["L0_xattn_bv", "L0_xattn_bo", "L1_xattn_bv", "L1_xattn_bo"]):
                for r in (0, 32):
                    sp.dma_start(bias_raw[r:r + 1, n, :], a[name].rearrange("(o p) -> o p", o=1)).then_inc(s["ld_s"], 16)
            sp.dma_start(gate_raw[:, 0, :], a["L0_ffn_w_gate"]).then_inc(s["ld_s"], 16)
            sp.dma_start(gate_raw[:, 1, :], a["L1_ffn_gate_w"]).then_inc(s["ld_s"], 16)
            for r in (HI_ROW, LO_ROW, HI2_ROW):
                sp.dma_start(b2_raw[r:r + EXPERTS, :], a["L1_ffn_b2"]).then_inc(s["ld_s"], 16)
            for g in range(GROUPS):
                sp.dma_start(x[:, G * g:G * (g + 1), :], x_dram[:, G * g:G * (g + 1), :]).then_inc((s["ld_x0"], s["ld_x1"], s["ld_x2"], s["ld_x3"])[g], 16)
            load_weights(1)
            for c in range(3):
                sp.dma_start(w_stage0[c].rearrange("p (a b) -> p a b", b=w_in[c].shape[2]), w_in[c]).then_inc(s["ch0_in"], 16)
            sp.dma_start(iota8[:, :], a["iota8"]).then_inc(s["cst"], 16)
            sp.dma_start(expert_rows[:, :], a["expert_rows"]).then_inc(s["cst"], 16)

            def load_chunk(c):
                sp.dma_start(w_stage[:, c % 2, :].rearrange("p (a b) -> p a b", b=chunks[c].shape[2]),
                             chunks[c]).then_inc((s["ch_in0"], s["ch_in1"])[c % 2], 16)

            load_chunk(0)
            load_chunk(1)

            def attention_operands(l):
                q = A[l]

                def tile_keys(t, par):
                    sp.dma_start(keys_now[:, par, :, :, :].rearrange("p a b k -> p (a b k)"),
                                 keys[:, t, :, :, :, :].rearrange("p a b j k -> p (a b j k)")).then_inc((q["kb0"], q["kb1"])[par], 16)

                def tile_vals(t, par):
                    sp.dma_start(vals_now[:, par, :, :, :, :].rearrange("p a b n v -> p a (b n v)"),
                                 vals[:, :, t, :, :, :, :].rearrange("p a b n h v -> p a (b n h v)")).then_inc((q["vb0"], q["vb1"])[par], 16)

                for n in (GROUPS * QUAD - 2, GROUPS * QUAD - 1):
                    wait_keys_split(sp, l, n)
                if l == 1:
                    sp.wait_ge(A[0]["s_ps"], 2 * TILES)
                    sp.wait_ge(A[0]["o_ps"], TILES)
                tile_keys(0, 0)
                tile_keys(1, 1)
                wait_values_split(sp, l, TILES // 2 - 1)
                for u in range(2):
                    sp.wait_ge(q["s_ps"], 2 * u + 2)
                    tile_keys(2 + u, u)
                    tile_vals(u, u)
                with sp.Fori(2, TILES // 2) as i:
                    for u in range(2):
                        sp.wait_ge(q["s_ps"], 4 * i + (2 * u - 2))
                        tile_keys(2 * i + u, u)
                        sp.wait_ge(q["o_ps"], 2 * i + (u - 3))
                        tile_vals(2 * i + (u - 2), u)
                for t in range(TILES - 2, TILES):
                    sp.wait_ge(q["o_ps"], t - 1)
                    tile_vals(t, t % 2)

            attention_operands(0)
            for c in range(2, len(chunks)):
                sp.wait_ge(s["ch_lo"], 3 + 2 * (c - 1))
                load_chunk(c)
            attention_operands(1)
            for g in range(GROUPS):
                sp.wait_ge(F[1]["res"], (EXPERTS - 1) * GROUPS + g + 1)
                sp.dma_start(out_dram[:, G * g:G * (g + 1), :], x[:, G * g:G * (g + 1), :]).then_inc(s["out_d"], 16)
            sp.wait_ge(s["out_d"], 16 * GROUPS)

        @block.scalar
        def _(act):
            act.wait_ge(s["ones"], 1)
            act.dma_start(quad_mask[:, :], a["quad_mask"]).then_inc(s["ld_k"], 16)
            for n, name in enumerate(["L0_xattn_bq", "L0_xattn_bk", "L1_xattn_bq", "L1_xattn_bk"]):
                act.dma_start(col_raw[N_B1 + n:N_B1 + n + 1, :], a[name].rearrange("(o p) -> o p", o=1)).then_inc(s["ld_k"], 16)
            act.dma_start(col_raw[0:N_B1, :], a["L1_ffn_b1"].rearrange("e (j p) -> (e j) p", p=P)).then_inc(s["ld_k"], 16)

            def weights_high(h):
                act.wait_ge(s["wt_ps"], h + 1)
                nc.scalar.activation(wT[:, 0, 4 * h:4 * h + 4, :], ps[:, WT_BANK[h], :].rearrange("p (a b) -> p a b", a=4),
                                     ACT.Copy, scale=WSCALE).then_inc(s["wt_hi"], 1)

            weights_high(0)
            for g in range(GROUPS):
                act.wait_ge(s["ct_ps"], g + 1)
                nc.scalar.activation(ctx_T[:, 0, g * GT:(g + 1) * GT], ps[:, 2 + g, :], ACT.Copy).then_inc(s["ct_hi"], 1)
            act.wait_ge(s["col_ps"], 1)
            nc.scalar.activation(cols[:, :], ps[:, 7, 0:P], ACT.Copy).then_inc(s["cols"], 1)

            def split_high(c):
                act.wait_ge(s["ch0_in"], 16 * 3)
                nc.scalar.activation(w_out[c][:, 0, :], w_stage0[c], ACT.Copy, scale=WSCALE).then_inc(s["ch_hi"], 1)

            def make_keys(l):
                q = KV[l]
                act.wait_ge(s["bkm"], l + 1)
                for g in range(GROUPS):
                    for j in range(QUAD):
                        n = QUAD * g + j
                        act.wait_ge(q["k_ps"], n + 1)
                        if n >= 4:
                            wait_keys_split(act, l, n - 4)
                        nc.scalar.activation(k_f[:, n % 4, :], ps[:, n % 2, :], ACT.Identity,
                                             bias=bk_m[:, l, j:j + 1], scale=1 / WSCALE).then_inc(q["k_f"], 1)
                        if n % 2 == 1:
                            act.wait_ge(q["k_f"], n)
                            nc.scalar.activation(keys[:, G * g:G * (g + 1), 0, :, j - 1, :],
                                                 k_f[:, (n - 1) % 4, :].rearrange("p (t b k) -> p t b k", t=G, b=PER_TILE),
                                                 ACT.Copy).then_inc(q["k_hi"], 1)

            def values(l, part):
                q = KV[l]
                if l == 0 and part == 0:
                    weights_high(1)
                for j in VALUE_PARTS[part]:
                    act.wait_ge(q["v_ps"], j + 1)
                    if j >= 2:
                        wait_values_split(act, l, j - 2)
                    nc.scalar.activation(v_f[:, j % 2, :], ps[:, 2 + j % 2, :], ACT.Copy,
                                         scale=1 / WSCALE).then_inc(q["v_f"], 1)
                    if l == 0 and j in LAYER0_SPLITS:
                        split_high(LAYER0_SPLITS.index(j))

            def attention(l):
                q = A[l]

                def step(t, u):
                    par = lambda k: (u + k) % 2 if not isinstance(t, int) else (t + k) % 2
                    if alive(t + 5):
                        act.wait_ge(q["xt_ps"], t + 6)
                        positive_wait(act, q["q_ps"], t + 4)
                        positive_wait(act, q["xt_lo"], t + 4)
                        nc.scalar.activation(xT_f[:, par(5), :], ps[:, 4, 0:P], ACT.Copy).then_inc(q["xt_hi"], 1)
                        nc.scalar.activation(xT[:, par(5), 0, :], ps[:, 4, 0:P], ACT.Copy).then_inc(q["xt_hi"], 1)
                    if alive(t + 4):
                        act.wait_ge(q["q_ps"], t + 5)
                        positive_wait(act, q["q_lo"], t + 3)
                        positive_wait(act, q["s_ps"], 2 * t + 6)
                        for n in range(QUADS):
                            r = slice(32 * n, 32 * n + 32)
                            nc.scalar.activation(q_f[r, par(4), n, :], ps[r, 7, 0:P], ACT.Identity,
                                                 bias=bias_col[r, 2 * l:2 * l + 1], scale=1 / WSCALE).then_inc(q["q_act"], 1)
                        act.wait_ge(q["q_act"], 5 * t + 24)
                        nc.scalar.activation(q_blk[:, par(4), 0, :, :], q_f[:, par(4), :, :], ACT.Copy).then_inc(q["q_act"], 1)
                    if alive(t + 3):
                        for h in range(2):
                            act.wait_ge(q["sub"], 2 * t + (7 + h))
                            r = slice(h * HALF, (h + 1) * HALF)
                            nc.scalar.activation(probs[:, par(3), r], probs[:, par(3), r], ACT.Exp,
                                                 scale=float(HD) ** -0.5).then_inc(q["ex"], 1)
                    if alive(t):
                        act.wait_ge(q["ot_ps"], t + 1)
                        positive_wait(act, q["y_ps"], t - 1)
                        nc.scalar.activation(oT[:, par(0), 0, :], ps[:, 6, 0:P], ACT.Copy).then_inc(q["ot_hi"], 1)
                    if alive(t + 2):
                        positive_wait(act, q["o_ps"], t + 1)
                        for h in range(2):
                            act.wait_ge(q["p_ps"], 2 * t + (5 + h))
                            nc.scalar.activation(pT[:, par(2), 0, 4 * h:4 * h + 4, :],
                                                 ps[:, 2 + h, :].rearrange("p (a b) -> p a b", a=4),
                                                 ACT.Copy).then_inc(q["p_hi"], 1)
                        positive_wait(act, q["p_lop"], t + 1)
                        nc.scalar.activation(p_f[:, par(2), :], ps[:, 3, :], ACT.Copy).then_inc(q["p_f"], 1)
                    if isinstance(t, int) and t in HIGH:
                        routing_high(F[l], HIGH.index(t))

                pipeline(act, step, TILES, 6, lambda n: values(l, n))

            def routing_high(q, g):
                act.wait_ge(q["xt_ps"], g + 1)
                nc.scalar.activation(xTa[:, 0, g * GT:(g + 1) * GT], ps[:, xta_bank[g], :], ACT.Copy).then_inc(q["xt_hi"], 1)

            def routing(l):
                q = F[l]
                routing_high(q, GROUPS - 1)
                act.wait_ge(q["pr"], 1)
                nc.scalar.activation(prob[:, :, 1], diff, ACT.Exp).then_inc(q["ex"], 1)
                nc.scalar.activation(act_warm[:, l:l + 1], minus_half[:, :], (ACT.Silu, ACT.Gelu)[l])
                if l == 0:
                    act.wait_ge(q["ct_ps"], 2)
                    nc.scalar.activation(combT[:, tokens // 2:tokens], half_bank[7], ACT.Copy).then_inc(q["ct_a"], 1)

            def experts0():
                q = F[0]
                with act.Fori(0, GROUPS // 2) as i:
                    for k in range(2 * STEPS0 + 1):
                        n = 2 * STEPS0 * i + k
                        if k < 2 * STEPS0:
                            act.wait_ge(q["up"], n + 1)
                            if k >= 4:
                                act.wait_ge(q["gt"], n - 3)
                            nc.scalar.activation(act_f[:, k % 4, :], ps[:, k % 2, :], ACT.Silu,
                                                 scale=1 / WSCALE).then_inc(q["act"], 1)
                        if k >= 1:
                            act.wait_ge(q["gt"], n)
                            if k >= 5:
                                act.wait_ge(q["down"], n - 4)
                            nc.scalar.activation(hid[:, (k - 1) % 4, 0, :], gated[:, (k - 1) % 4, :],
                                                 ACT.Copy).then_inc(q["hi"], 1)
                        if k in CHUNK_STEPS:
                            m = CHUNK_STEPS.index(k)
                            act.wait_ge((s["ch_in0"], s["ch_in1"])[m % 2], 32 * i + 16 * (m // 2 + 1))
                            nc.scalar.activation(w12[:, 0, 4 * i + m, :], w_stage[:, m % 2, :],
                                                 ACT.Copy, scale=WSCALE).then_inc(s["ch_hi"], 1)

            def experts1():
                q = F[1]
                K = GROUPS * STEPS1

                def expert(e):
                    nc.scalar.activation(b1_now[:, :], b1_col[:, e, :], ACT.Copy).then_inc(q["b1"], 1)
                    act.wait_ge(q["b1"], e + 1)
                    for k in range(K):
                        n = K * e + k
                        act.wait_ge(q["up"], n + 1)
                        positive_wait(act, q["lo"], n - 3)
                        nc.scalar.activation(act_f[:, k % 4, :], ps[:, k % 4, :], ACT.Gelu,
                                             bias=b1_now[:, k % STEPS1:k % STEPS1 + 1], scale=1 / WSCALE).then_inc(q["act"], 1)
                        act.wait_ge(q["act"], n + 1)
                        positive_wait(act, q["down"], n - 3)
                        nc.scalar.activation(hid[:, k % 4, 0, :], act_f[:, k % 4, :], ACT.Copy).then_inc(q["hi"], 1)

                expert(0)
                with act.Fori(1, EXPERTS) as e:
                    expert(e)

            make_keys(0)
            act.wait_ge(s["zero"], 5)
            attention(0)
            routing(0)
            experts0()
            act.wait_ge(F[0]["res"], GROUPS + 1)
            make_keys(1)
            attention(1)
            routing(1)
            experts1()

        @block.gpsimd
        def _(pool):
            nc.gpsimd.memset(minus_half[:, :], -0.5).then_inc(s["zero"], 1)
            nc.gpsimd.memset(wk_m[:, :, :, :, :].bitcast(F32), 0.0).then_inc(s["zero"], 1)
            nc.gpsimd.memset(vals_flat[:, :].bitcast(F32), 0.0).then_inc(s["zero"], 1)
            nc.gpsimd.memset(q_f[:, :, :, :], 0.0).then_inc(s["zero"], 1)
            nc.gpsimd.memset(comb16.rearrange("p t c -> p (t c)").bitcast(F32), 0.0).then_inc(s["zero"], 1)

            def rstds(t, width, n, slot=0):
                pool.wait_ge(s["agg"], n + width)
                nc.gpsimd.tensor_tensor(mv[:, bass.ds(t, width), :], mv_now[:, slot:slot + width, :],
                                        zero_eps[:, :].unsqueeze(1).broadcast_to([P, width, 2]), ALU.add).then_inc(s["ag"], width)
                pool.wait_ge(s["ag"], n + width)
                nc.gpsimd.tensor_tensor(rstd[:, bass.ds(t, width)], mv[:, bass.ds(t, width), 1:2].rearrange("p a o -> p (a o)"),
                                        minus_half[:, 0:1].broadcast_to([P, width]), ALU.pow).then_inc(s["rs"], width)

            def make_keys(l):
                q = KV[l]
                for g in range(GROUPS):
                    for j in range(0, QUAD, 2):
                        n = QUAD * g + j
                        pool.wait_ge(q["k_hi"], n // 2 + 1)
                        hi, lo = (keys[:, G * g:G * (g + 1), c, :, j, :] for c in range(2))
                        f = k_f[:, n % 4, :].rearrange("p (t b k) -> p t b k", t=G, b=PER_TILE)
                        nc.gpsimd.tensor_tensor(lo, f, hi, ALU.subtract).then_inc(q["pool"], 1)
                    if l == 0:
                        pool.wait_ge(q["pool"], 2 * (g + 1))
                        rstds(G * g, G, G * g)
                        pool.wait_ge(s["rs"], G * (g + 1))
                pool.wait_ge(q["pool"], GROUPS * QUAD // 2)

            def values(l, part):
                q = KV[l]
                if part == 1:
                    pool.wait_ge(A[l]["xt_lo"], 1)
                if part == 2:
                    pool.wait_ge(A[l]["q_lo"], 1)
                for j in VALUE_PARTS[part]:
                    pool.wait_ge(q["v_w"], 3 * j + 2)
                    pool.wait_ge(q["pool"], GROUPS * QUAD // 2 + j)
                    hi, lo, f = value_parts(j, 1)
                    nc.gpsimd.tensor_tensor(lo, f, hi, ALU.subtract).then_inc(q["pool"], 1)
                pool.wait_ge(q["pool"], GROUPS * QUAD // 2 + VALUE_PARTS[part][-1] + 1)

            def attention(l):
                q = A[l]

                def step(t, u):
                    par = lambda k: (u + k) % 2 if not isinstance(t, int) else (t + k) % 2
                    if alive(t + 5):
                        pool.wait_ge(q["xt_hi"], 2 * t + 12)
                        positive_wait(pool, q["q_ps"], t + 4)
                        positive_wait(pool, q["p_lop"], t + 2)
                        positive_wait(pool, q["q_lo"], t + 4)
                        nc.gpsimd.tensor_tensor(xT[:, par(5), 1, :], xT_f[:, par(5), :], xT[:, par(5), 0, :],
                                                ALU.subtract).then_inc(q["xt_lo"], 1)
                    if alive(t + 4):
                        pool.wait_ge(q["q_act"], 5 * t + 25)
                        positive_wait(pool, q["s_ps"], 2 * t + 6)
                        positive_wait(pool, q["p_lop"], t + 2)
                        pool.wait_ge(q["xt_lo"], within(t + 6))
                        nc.gpsimd.tensor_tensor(q_blk[:, par(4), 1, :, :].rearrange("p n c -> p (n c)"), q_f[:, par(4), :, :].rearrange("p n c -> p (n c)"),
                                                q_blk[:, par(4), 0, :, :].rearrange("p n c -> p (n c)"), ALU.subtract).then_inc(q["q_lo"], 1)
                    if alive(t - 1):
                        pool.wait_ge(q["q_lo"], within(t + 5))
                        rstds(t - 1, 1, t + ((2 * l + 1) * TILES - 1), par(1))
                    if alive(t + 2):
                        pool.wait_ge(q["p_f"], t + 3)
                        pool.wait_ge(q["p_hi"], 2 * t + 6)
                        positive_wait(pool, q["o_ps"], t + 1)
                        pool.wait_ge(q["q_lo"], within(t + 5))
                        pool.wait_ge(s["rs"], max(t, 0) + (2 * l + 1) * TILES if isinstance(t, int) else t + (2 * l + 1) * TILES)
                        nc.gpsimd.tensor_tensor(pT[:, par(2), 1, 4:8, :].rearrange("p a b -> p (a b)"), p_f[:, par(2), :],
                                                pT[:, par(2), 0, 4:8, :].rearrange("p a b -> p (a b)"), ALU.subtract).then_inc(q["p_lop"], 1)

                pipeline(pool, step, TILES, 6, lambda n: values(l, n))

            pool.wait_ge(s["zero"], 5)
            pool.wait_ge(s["ones"], 2)
            make_keys(0)
            attention(0)
            pool.wait_ge(s["rs"], 2 * TILES)
            q = F[0]
            with pool.Fori(0, GROUPS // 2) as i:
                for k in range(2 * STEPS0):
                    n = 2 * STEPS0 * i + k
                    pool.wait_ge(q["hi"], n + 1)
                    nc.gpsimd.tensor_tensor(hid[:, k % 4, 1, :], gated[:, k % 4, :], hid[:, k % 4, 0, :],
                                            ALU.subtract).then_inc(q["lo"], 1)
                    if k == STEPS0 + 5:
                        rstds(8 * i, G, 8 * i + 2 * TILES)
                rstds(8 * i + 4, G, 8 * i + (2 * TILES + 4))
            pool.wait_ge(s["rs"], 3 * TILES)
            make_keys(1)
            attention(1)

        @block.vector
        def _(dve):
            def carry_wait():
                nc.vector.tensor_copy(wait_carrier[:, 1:2], wait_carrier[:, 0:1])

            def spread(t, slot):
                nc.vector.bn_stats(stats[:, slot, :], x[:, t, :]).then_inc(s["st"], 1)

            def mean_var(slot):
                nc.vector.bn_aggr(mv_now[:, slot, :], stats[:, slot, :]).then_inc(s["agg"], 1)

            nc.vector.memset(col_raw[:, :], 0.0).then_inc(s["ones"], 1)
            nc.vector.memset(zero_eps[:, 0:1], 0.0)
            nc.vector.memset(wait_carrier[:, :], 0.0).then_inc(s["ones"], 1)
            nc.vector.memset(zero_eps[:, 1:2], EPS).then_inc(s["ones"], 1)
            nc.vector.memset(bias_rows[:, :, :], 0.0).then_inc(s["ones"], 1)
            nc.vector.memset(b2_rows[:, :], 0.0).then_inc(s["ones"], 1)
            dve.wait_ge(s["ones"], 5)

            def weights_low(h):
                dve.wait_ge(s["wt_hi"], h + 1)
                nc.vector.scalar_tensor_tensor(wT[:, 1, 4 * h:4 * h + 4, :].rearrange("p a b -> p (a b)"), ps[:, WT_BANK[h], :], WSCALE,
                                               wT[:, 0, 4 * h:4 * h + 4, :].rearrange("p a b -> p (a b)"),
                                               ALU.mult, ALU.subtract).then_inc(s["wt_lo"], 1)
                dve.wait_ge(s["wt_lo"], h + 1)
                dve.wait_ge(s["zero"], 2)
                for i in range(2):
                    for j in range(QUAD):
                        c = slice(j * HD, (j + 1) * HD)
                        nc.vector.tensor_copy(wk_m[:, h, i, j, :].rearrange("p (g c) -> p g c", g=QUADS)[:, :, c],
                                              wT[:, i, 4 * h + 1, :].rearrange("p (g c) -> p g c", g=QUADS)[:, :, c]).then_inc(s["msk"], 1)

            def key_bias(l):
                nc.vector.tensor_scalar(bk_m[:, l, :], quad_mask[:, :], bias_col[:, 2 * l + 1:2 * l + 2], None,
                                        ALU.mult).then_inc(s["bkm"], 1)

            def group_statistics(g):
                dve.wait_ge((s["ld_x0"], s["ld_x1"], s["ld_x2"], s["ld_x3"])[g], 16)
                positive_wait(dve, s["agg"], G * g)
                for t in range(G):
                    spread(G * g + t, t)
                dve.wait_ge(s["st"], G * g + G)
                positive_wait(dve, s["ag"], G * g)
                for t in range(G):
                    mean_var(t)

            weights_low(0)
            for g in range(GROUPS):
                dve.wait_ge(s["ct_hi"], g + 1)
                r = slice(g * GT, (g + 1) * GT)
                nc.vector.tensor_tensor(ctx_T[:, 1, r], ps[:, 2 + g, :], ctx_T[:, 0, r], ALU.subtract).then_inc(s["ct_lo"], 1)
            dve.wait_ge(s["ld_k"], 16 * 6)
            dve.wait_ge(s["cols"], 1)
            for l in range(2):
                key_bias(l)
            dve.wait_ge(s["zero"], 3)
            for h2 in range(2):
                r = slice(64 * h2, 64 * h2 + 64)
                nc.vector.memset(vals[r, 0, :, :, :, h2, HD:VW].rearrange("p t b a o -> p (t b a) o"), 1.0)
            nc.vector.tensor_copy(ident16[:, :], ident[:, :])

            def small_operands():
                dve.wait_ge(s["ld_s"], 16 * (1 + 8 + 2 + 3))
                nc.vector.tensor_scalar(bias_rows[0:1, :, :], bias_raw[0:1, :, :], WSCALE, None, ALU.mult).then_inc(s["small_hi"], 1)
                nc.vector.tensor_scalar(bias_hi[32:33, :, :], bias_raw[32:33, :, :], WSCALE, None, ALU.mult).then_inc(s["small_hi"], 1)
                for r in (HI_ROW, LO_ROW):
                    nc.vector.tensor_scalar(b2_rows[r:r + EXPERTS, :], b2_raw[r:r + EXPERTS, :], WSCALE, None, ALU.mult).then_inc(s["small_hi"], 1)
                r = slice(HI2_ROW, HI2_ROW + EXPERTS)
                nc.vector.tensor_scalar(b2_hi[r, :], b2_raw[r, :], WSCALE, None, ALU.mult).then_inc(s["small_hi"], 1)
                for l in range(2):
                    nc.vector.tensor_scalar(gate_w[:, l, 0, :], gate_raw[:, l, :], WSCALE, None, ALU.mult).then_inc(s["small_hi"], 1)
                dve.wait_ge(s["small_hi"], 7)
                nc.vector.scalar_tensor_tensor(bias_rows[32:33, :, :], bias_raw[32:33, :, :], WSCALE, bias_hi[32:33, :, :],
                                               ALU.mult, ALU.subtract).then_inc(s["small_lo"], 1)
                nc.vector.scalar_tensor_tensor(b2_rows[r, :], b2_raw[r, :], WSCALE, b2_hi[r, :], ALU.mult, ALU.subtract).then_inc(s["small_lo"], 1)
                for l in range(2):
                    nc.vector.scalar_tensor_tensor(gate_w[:, l, 1, :], gate_raw[:, l, :], WSCALE, gate_w[:, l, 0, :],
                                                   ALU.mult, ALU.subtract).then_inc(s["small_lo"], 1)

            def make_keys(l):
                q = KV[l]
                for g in range(GROUPS):
                    for j in range(QUAD):
                        n = QUAD * g + j
                        hi, lo = (keys[:, G * g:G * (g + 1), c, :, j, :] for c in range(2))
                        f = k_f[:, n % 4, :].rearrange("p (t b k) -> p t b k", t=G, b=PER_TILE)
                        if n % 2 == 1:
                            dve.wait_ge(q["k_f"], n + 1)
                            nc.vector.tensor_copy(hi, f).then_inc(q["k_dve"], 1)
                            dve.wait_ge(q["k_dve"], n)
                            nc.vector.tensor_tensor(lo, f, hi, ALU.subtract).then_inc(q["k_dve"], 1)
                    if l == 0:
                        group_statistics(g)
                    if l == 0 and g == 1:
                        small_operands()

            def values(l, part):
                q = KV[l]
                for j in VALUE_PARTS[part]:
                    dve.wait_ge(q["v_f"], j + 1)
                    if l == 1 and j == 0:
                        dve.wait_ge(A[0]["o_ps"], TILES)
                    parts = []
                    for h2 in range(2):
                        parts.append(value_parts(j, h2))
                    for hi, lo, f in parts:
                        nc.vector.tensor_copy(hi, f).then_inc(q["v_w"], 1)
                    dve.wait_ge(q["v_w"], 3 * j + 1)
                    hi, lo, f = parts[0]
                    nc.vector.tensor_tensor(lo, f, hi, ALU.subtract).then_inc(q["v_w"], 1)
                    if l == 0 and j in LAYER0_SPLITS:
                        chunk0_low(LAYER0_SPLITS.index(j))

            def attention(l):
                q = A[l]
                inv = 1 / WSCALE

                def step(t, u):
                    par = lambda k: (u + k) % 2 if not isinstance(t, int) else (t + k) % 2
                    if alive(t + 3):
                        hh = HEADS // 2
                        for h in range(2):
                            dve.wait_ge(q["s_ps"], 2 * t + (7 + h))
                            positive_wait(dve, q["sub"], 2 * t + (3 + h))
                            nc.vector.tensor_reduce(mx[:, par(3), h * hh:(h + 1) * hh], ps[:, h, :].rearrange("p (h k) -> p h k", k=SEQ),
                                                    axis=AX.X, op=ALU.max).then_inc(q["mx"], 1)
                    if l == 0 and isinstance(t, int) and t == -2:
                        weights_low(1)
                    if alive(t + 6):
                        dve.wait_ge(s["rs"], t + (7 + 2 * l * TILES))
                        positive_wait(dve, q["xt_ps"], t + 5)
                        nc.vector.tensor_scalar(xhat[:, par(6), :], x[:, t + 6, :], mv[:, t + 6, 0:1],
                                                rstd[:, t + 6:t + 7] if isinstance(t, int) else rstd[:, bass.ds(t + 6, 1)],
                                                ALU.subtract, ALU.mult).then_inc(q["xh"], 1)
                    if alive(t + 3):
                        for h in range(2):
                            dve.wait_ge(q["mx"], 2 * t + (7 + h))
                            positive_wait(dve, q["p_ps"], 2 * t + (3 + h))
                            nc.vector.tensor_tensor(
                                probs[:, par(3), h * HALF:(h + 1) * HALF].rearrange("p (h k) -> p h k", k=SEQ),
                                ps[:, h, :].rearrange("p (h k) -> p h k", k=SEQ),
                                mx[:, par(3), h * hh:(h + 1) * hh].unsqueeze(2).broadcast_to([P, hh, SEQ]),
                                ALU.subtract).then_inc(q["sub"], 1)
                    if alive(t + 1):
                        dve.wait_ge(q["o_ps"], t + 2)
                        positive_wait(dve, q["ot_ps"], t)
                        o = ps[:, 5, 0:PAIRS * PER_TILE * 2 * VW].rearrange("p (a b h v) -> p a b h v", b=2, h=2, v=VW)
                        nc.vector.reciprocal(rden[:, par(1), :].rearrange("p (a h) -> p a h", h=2), o[:, :, 0, :, HD]).then_inc(q["rd"], 1)
                    if alive(t - 1):
                        dve.wait_ge(q["y_ps"], t)
                        at = t - 1 if isinstance(t, int) else bass.ds(t - 1, 1)
                        xt = x[:, at, :] if isinstance(t, int) else x[:, at, :].rearrange("p o d -> p (o d)")
                        nc.vector.scalar_tensor_tensor(xt, ps[:, 7, P:2 * P], inv, xt, ALU.mult, ALU.add).then_inc(q["res"], 1)
                    if alive(t + 1):
                        dve.wait_ge(q["rd"], t + 2)
                        for b in range(PER_TILE):
                            rows = slice(64 * b, 64 * b + 64)
                            nc.vector.tensor_tensor(
                                o_n[rows, par(1), :].rearrange("p (a h v) -> p a h v", h=2, v=HD), o[rows, :, b, :, 0:HD],
                                rden[rows, par(1), :].rearrange("p (a h o) -> p a h o", h=2, o=1).broadcast_to([64, PAIRS, 2, HD]),
                                ALU.mult).then_inc(q["on"], 1)
                    if alive(t - 1):
                        dve.wait_ge(q["res"], t)
                        dve.wait_ge(s["agg"], t + ((2 * l + 1) * TILES - 2))
                        carry_wait()
                        spread(t - 1, par(1))
                    if alive(t):
                        dve.wait_ge(q["ot_hi"], t + 1)
                        positive_wait(dve, q["y_ps"], t - 1)
                        nc.vector.tensor_tensor(oT[:, par(0), 1, :], ps[:, 6, 0:P], oT[:, par(0), 0, :],
                                                ALU.subtract).then_inc(q["ot_lo"], 1)
                    if alive(t - 1):
                        dve.wait_ge(s["st"], t + (2 * l + 1) * TILES)
                        dve.wait_ge(s["ag"], t + ((2 * l + 1) * TILES - 2))
                        carry_wait()
                        mean_var(par(1))
                    if alive(t + 2):
                        positive_wait(dve, q["o_ps"], t + 1)
                        dve.wait_ge(q["p_hi"], 2 * t + 5)
                        nc.vector.tensor_tensor(pT[:, par(2), 1, 0:4, :].rearrange("p a b -> p (a b)"), ps[:, 2, :],
                                                pT[:, par(2), 0, 0:4, :].rearrange("p a b -> p (a b)"), ALU.subtract).then_inc(q["p_lo"], 1)

                    if isinstance(t, int) and t in RANK:
                        rank(F[l], RANK.index(t))
                    if isinstance(t, int) and t in LOW:
                        low(F[l], LOW.index(t))
                    if isinstance(t, int) and t in NORMALISE:
                        normalise(l, NORMALISE.index(t))

                pipeline(dve, step, TILES, 6, lambda n: values(l, n))

            def chunk0_low(c):
                dve.wait_ge(s["ch_hi"], c + 1)
                nc.vector.scalar_tensor_tensor(w_out[c][:, 1, :], w_stage0[c], WSCALE, w_out[c][:, 0, :],
                                               ALU.mult, ALU.subtract).then_inc(s["ch_lo"], 1)

            def routing(l):
                q = F[l]
                normalise(l, GROUPS - 1)
                rank(q, GROUPS - 2)
                low(q, GROUPS - 1)
                rank(q, GROUPS - 1)
                dve.wait_ge(q["top"], TILES)
                nc.vector.tensor_tensor(diff, top_v[:, :, 1], top_v[:, :, 0], ALU.subtract).then_inc(q["pr"], 1)
                dve.wait_ge(q["idx"], TILES)
                nc.vector.tensor_copy(top_f, top_i[:, :, 0:2]).then_inc(q["idx"], 1)
                dve.wait_ge(q["idx"], TILES + 1)
                dve.wait_ge(s["cst"], 32)
                for c in range(2):
                    nc.vector.tensor_tensor(one_hot[:, c, :, :], iota8[:, :].unsqueeze(1).broadcast_to([P, TILES, EXPERTS]),
                                            top_f[:, :, c:c + 1].broadcast_to([P, TILES, EXPERTS]), ALU.is_equal).then_inc(q["oh"], 1)
                dve.wait_ge(q["ex"], 1)
                nc.vector.tensor_scalar(diff, prob[:, :, 1], 1.0, None, ALU.add).then_inc(q["pr"], 1)
                dve.wait_ge(q["pr"], 2)
                nc.vector.reciprocal(prob[:, :, 0], diff).then_inc(q["pr"], 1)
                dve.wait_ge(q["pr"], 3)
                nc.vector.tensor_tensor(prob[:, :, 1], prob[:, :, 1], prob[:, :, 0], ALU.mult).then_inc(q["pr"], 1)
                dve.wait_ge(q["pr"], 4)
                dve.wait_ge(q["oh"], 2)
                for c in range(2):
                    nc.vector.tensor_tensor(one_hot[:, c, :, :], one_hot[:, c, :, :],
                                            prob[:, :, c:c + 1].broadcast_to([P, TILES, EXPERTS]), ALU.mult).then_inc(q["oh"], 1)
                dve.wait_ge(q["oh"], 4)
                nc.vector.tensor_tensor(comb, one_hot[:, 0, :, :], one_hot[:, 1, :, :], ALU.add).then_inc(q["cb"], 1)
                dve.wait_ge(q["cb"], 1)
                for col in (HI_ROW, HI2_ROW):
                    nc.vector.tensor_copy(comb16[:, :, col:col + EXPERTS], comb).then_inc(q["c16"], 1)
                dve.wait_ge(q["c16"], 2)
                nc.vector.tensor_tensor(comb16[:, :, LO_ROW:LO_ROW + EXPERTS], comb, comb16[:, :, HI_ROW:HI_ROW + EXPERTS],
                                        ALU.subtract).then_inc(q["c16"], 1)
                for h in range(1 + l):
                    dve.wait_ge(q["ct_ps"], h + 1)
                    r = slice(h * tokens // 2, (h + 1) * tokens // 2)
                    nc.vector.tensor_copy(combT[:, r], half_bank[6 + h]).then_inc(q["ct_d"], 1)

            def normalise(l, g):
                q = F[l]
                if g >= 2:
                    dve.wait_ge(q["xt_ps"], g - 1)
                for t in range(G * g, G * g + G):
                    dve.wait_ge(s["rs"], t + (1 + (2 * l + 1) * TILES))
                    nc.vector.tensor_scalar(fx[:, g % 2, (t % G) * P:(t % G + 1) * P], x[:, t, :], mv[:, t, 0:1], rstd[:, t:t + 1],
                                            ALU.subtract, ALU.mult).then_inc(q["xh"], 1)

            def rank(q, g):
                dve.wait_ge(q["lg_ps"], g + 1)
                r = slice(G * g, G * g + G)
                nc.vector.tensor_scalar(logits[:, r, :], ps[:, logit_bank[g % 2], G * g * EXPERTS:G * (g + 1) * EXPERTS].rearrange("p (t e) -> p t e", e=EXPERTS),
                                        1 / WSCALE, None, ALU.mult).then_inc(q["lg"], 1)
                dve.wait_ge(q["lg"], g + 1)
                for t in range(G * g, G * g + G):
                    nc.vector.max(top_v[:, t, :], logits[:, t, :]).then_inc(q["top"], 1)
                for t in range(G * g, G * g + G):
                    dve.wait_ge(q["top"], t + 1)
                    nc.vector.max_index(top_i[:, t, :], top_v[:, t, :], logits[:, t, :]).then_inc(q["idx"], 1)

            def low(q, g):
                dve.wait_ge(q["xt_hi"], g + 1)
                r = slice(g * GT, (g + 1) * GT)
                nc.vector.tensor_tensor(xTa[:, 1, r], ps[:, xta_bank[g], :], xTa[:, 0, r], ALU.subtract).then_inc(q["xt_lo"], 1)

            def experts0():
                q = F[0]
                nc.vector.memset(wait_carrier[:, :], 0.0).then_inc(q["res"], 1)
                with dve.Fori(0, GROUPS // 2) as i:
                    for k in range(2 * STEPS0):
                        n = 2 * STEPS0 * i + k
                        dve.wait_ge(q["act"], n + 1)
                        nc.vector.scalar_tensor_tensor(act_f[:, k % 4, :], ps[:, 2 + k % 2, :], 1 / WSCALE, act_f[:, k % 4, :],
                                                       ALU.mult, ALU.mult).then_inc(q["t1"], 1)
                        dve.wait_ge(q["t1"], n + 1)
                        if k >= 4:
                            dve.wait_ge(q["lo"], n - 3)
                        nc.vector.tensor_tensor(gated[:, k % 4, :], ps[:, 4 + k % 2, :], act_f[:, k % 4, :], ALU.mult).then_inc(q["gt"], 1)
                        for h in range(2):
                            if k - h in CHUNK_STEPS:
                                m = CHUNK_STEPS.index(k - h)
                                dve.wait_ge(s["ch_hi"], 4 * i + (3 + m + 1))
                                r = slice(h * M1, (h + 1) * M1)
                                nc.vector.scalar_tensor_tensor(w12[:, 1, 4 * i + m, r], w_stage[:, m % 2, r], WSCALE,
                                                               w12[:, 0, 4 * i + m, r], ALU.mult, ALU.subtract).then_inc(s["ch_lo"], 1)
                        if k == STEPS0 + 4:
                            residual0(i, 0)
                    residual0(i, 1)

            def residual0(i, half):
                q = F[0]
                gi = 2 * i + half
                dve.wait_ge(q["down"], 2 * STEPS0 * i + STEPS0 * (half + 1))
                nc.vector.scalar_tensor_tensor(
                    x[:, bass.ds(8 * i + 4 * half, G), :].rearrange("p t d -> p (t d)"), ps[:, 6 + half, :], 1 / WSCALE,
                    x[:, bass.ds(8 * i + 4 * half, G), :].rearrange("p t d -> p (t d)"), ALU.mult, ALU.add).then_inc(q["res"], 1)
                n = 2 * TILES + 8 * i + 4 * half
                dve.wait_ge(q["res"], gi + 2)
                dve.wait_ge(s["agg"], n)
                carry_wait()
                for t in range(G):
                    spread(8 * i + (4 * half + t), t)
                dve.wait_ge(s["st"], n + G)
                dve.wait_ge(s["ag"], n)
                carry_wait()
                for t in range(G):
                    mean_var(t)

            def experts1():
                q = F[1]
                BIAS_STEPS = (1, 2, 4, 5)

                def output_biases(g):
                    dve.wait_ge(q["b2_ps"], g + 1)
                    r = x[:, G * g:G * (g + 1), :].rearrange("p t d -> p (t d)")
                    nc.vector.scalar_tensor_tensor(r, ps[:, 6 + g % 2, :], 1 / WSCALE, r, ALU.mult, ALU.add).then_inc(q["b2_r"], 1)

                dve.wait_ge(q["c16"], 3)
                nc.vector.tensor_scalar(comb, comb, 1 / WSCALE, None, ALU.mult).then_inc(q["cb"], 1)
                dve.wait_ge(q["cb"], 2)
                K = GROUPS * STEPS1

                def expert(e):
                    for k in range(K):
                        n = K * e + k
                        dve.wait_ge(q["hi"], n + 1)
                        positive_wait(dve, q["down"], n - 3)
                        nc.vector.tensor_tensor(hid[:, k % 4, 1, :], act_f[:, k % 4, :], hid[:, k % 4, 0, :], ALU.subtract).then_inc(q["lo"], 1)
                        if isinstance(e, int) and k in BIAS_STEPS:
                            output_biases(BIAS_STEPS.index(k))
                        if isinstance(e, int) and k == STEPS1 + 2:
                            dve.wait_ge(q["b2_r"], GROUPS)
                        if k % STEPS1 == 2:
                            if k > STEPS1:
                                accumulate(e, k // STEPS1 - 1, GROUPS * e + k // STEPS1)
                            elif not isinstance(e, int):
                                accumulate(e - 1, GROUPS - 1, GROUPS * e)

                expert(0)
                with dve.Fori(1, EXPERTS) as e:
                    expert(e)
                accumulate(EXPERTS - 1, GROUPS - 1, GROUPS * EXPERTS)

            def accumulate(e, g, done):
                q = F[1]
                dve.wait_ge(q["down"], STEPS1 * done)
                for t in range(G):
                    ins = nc.vector.scalar_tensor_tensor(x[:, G * g + t, :], ps[:, 4 + g % 2, t * P:(t + 1) * P],
                                                         comb[:, G * g + t, bass.ds(e, 1)], x[:, G * g + t, :], ALU.mult, ALU.add)
                ins.then_inc(q["res"], 1)

            make_keys(0)
            attention(0)
            routing(0)
            experts0()
            make_keys(1)
            attention(1)
            routing(1)
            experts1()

        @block.tensor
        def _(pe):
            def three(dst, lhs, rhs, start=True, stop=True, **kw):
                pe.matmul(dst, lhs[0], rhs[0], start=start, stop=False, **kw)
                pe.matmul(dst, lhs[0], rhs[1], start=False, stop=False, **kw)
                return pe.matmul(dst, lhs[1], rhs[0], start=False, stop=stop, **kw)

            pe.wait_ge(s["ids"], 16)
            def transpose_weights(h):
                pe.wait_ge((s["ld_w0"], s["ld_w1"])[h], 16 * 4)
                for n in range(4):
                    mm = pe.transpose(ps[:, WT_BANK[h], n * P:(n + 1) * P], w_raw[:, 4 * h + n, :], ident[:, :])
                mm.then_inc(s["wt_ps"], 1)

            transpose_weights(0)
            pe.wait_ge(s["ld_c"], 16 * GROUPS)
            for g in range(GROUPS):
                for n in range(G):
                    mm = pe.transpose(ps[:, 2 + g, n * P:(n + 1) * P], ctx_raw[:, G * g + n, :], ident[:, :])
                mm.then_inc(s["ct_ps"], 1)
            pe.wait_ge(s["ld_k"], 16 * 6)
            pe.transpose(ps[:, 7, 0:P], col_raw[:, :], ident[:, :]).then_inc(s["col_ps"], 1)

            def W(l, which):
                n = 4 * l + "qkvo".index(which)
                return wT[:, 0, n, :], wT[:, 1, n, :]

            def make_keys(l):
                q = KV[l]
                pe.wait_ge(s["msk"], 2 * QUAD * (l + 1))
                for g in range(GROUPS):
                    pe.wait_ge(s["ct_lo"], g + 1)
                    if l == 0 and g == 2:
                        transpose_weights(1)
                    r = slice(g * GT, (g + 1) * GT)
                    for j in range(QUAD):
                        n = QUAD * g + j
                        if n >= 2:
                            pe.wait_ge(q["k_f"], n - 1)
                        three(ps[:, n % 2, :], (wk_m[:, l, 0, j, :], wk_m[:, l, 1, j, :]),
                              (ctx_T[:, 0, r], ctx_T[:, 1, r])).then_inc(q["k_ps"], 1)

            def values(l, part):
                q = KV[l]
                wv = W(l, "v")
                pe.wait_ge(s["small_lo"], 1)
                for j in VALUE_PARTS[part]:
                    if j >= 2:
                        pe.wait_ge(q["v_f"], j - 1)
                    for n in range(4):
                        c = [ctx_T[:, i, (4 * j + n) * SEQ:(4 * j + n + 1) * SEQ] for i in range(2)]
                        cols_n = slice(n * P, (n + 1) * P)
                        pe.matmul(ps[:, 2 + j % 2, cols_n], two_rows[:, :], bias_rows[:, 2 * l, :], start=True, stop=False)
                        for ci, wi in ((0, 0), (0, 1), (1, 0)):
                            for h2 in range(2):
                                mm = pe.matmul(ps[64 * h2:64 * h2 + 64, 2 + j % 2, cols_n], c[ci], wv[wi], start=False, stop=(ci == 1))
                    mm.then_inc(q["v_ps"], 1)

            def attention(l):
                q = A[l]
                pe.wait_ge(s["bkm"], 2)

                def step(t, u):
                    par = lambda k: (u + k) % 2 if not isinstance(t, int) else (t + k) % 2
                    if alive(t + 4):
                        pe.wait_ge(q["xt_lo"], t + 5)
                        positive_wait(pe, q["q_act"], 5 * t + 20)
                        positive_wait(pe, q["res"], t - 1)
                        three(ps[:, 7, 0:P], W(l, "q"), (xT[:, par(4), 0, :], xT[:, par(4), 1, :])).then_inc(q["q_ps"], 1)
                    if alive(t + 5):
                        pe.wait_ge(q["xh"], t + 6)
                        positive_wait(pe, q["xt_lo"], t + 5)
                        pe.transpose(ps[:, 4, 0:P], xhat[:, par(5), :], ident[:, :]).then_inc(q["xt_ps"], 1)
                    if alive(t + 3):
                        pr = par(3)
                        pe.wait_ge(q["q_lo"], t + 4)
                        if isinstance(t, int):
                            pe.wait_ge((q["kb0"], q["kb1"])[pr], 16 * ((t + 3) // 2 + 1))
                        else:
                            pe.wait_ge((q["kb0"], q["kb1"])[pr], 8 * t + (32 + 8 * u))
                        for n in range(QUADS):
                            if n % 2 == 0:
                                positive_wait(pe, q["sub"], 2 * t + (5 + n // 2))
                            for qi, ki in ((0, 0), (0, 1), (1, 0)):
                                for b in range(PER_TILE):
                                    c = QUAD * SEQ * (n % 2)
                                    mm = pe.matmul(ps[64 * b:64 * b + 64, n // 2, c:c + QUAD * SEQ], q_blk[:, pr, qi, n, 64 * b:64 * b + 64],
                                                   keys_now[:, pr, ki, b, :], start=(qi + ki == 0), stop=(qi == 1))
                            if n % 2 == 1:
                                mm.then_inc(q["s_ps"], 1)
                    if alive(t + 1):
                        positive_wait(pe, q["on"], 2 * t + 2)
                        pe.wait_ge(q["p_lo"], t + 2)
                        pr = par(1)
                        pe.wait_ge((q["vb0"], q["vb1"])[pr], 16 * ((t + 1) // 2 + 1) if isinstance(t, int) else 8 * t + (16 + 8 * u))
                        pe.wait_ge(q["p_lop"], t + 2)
                        for n in range(PAIRS):
                            w = PER_TILE * 2 * VW
                            v = [vals_now[:, pr, i, :, n, :] for i in range(2)]
                            mm = three(ps[:, 5, n * w:(n + 1) * w].rearrange("p (b v) -> p b v", b=PER_TILE), (pT[:, par(1), 0, n, :], pT[:, par(1), 1, n, :]), v)
                        mm.then_inc(q["o_ps"], 1)
                    if alive(t):
                        pe.wait_ge(q["on"], 2 * t + 2)
                        if l == 0 and isinstance(t, int) and t == 0:
                            pe.wait_ge(s["wt_lo"], 2)
                        positive_wait(pe, q["ot_lo"], t)
                        pe.transpose(ps[:, 6, 0:P], o_n[:, par(0), :], ident[:, :]).then_inc(q["ot_ps"], 1)
                    if alive(t - 1):
                        pe.wait_ge(q["ot_lo"], t)
                        positive_wait(pe, q["res"], t - 1)
                        pe.wait_ge(q["q_act"], 5 * within(t + 5))
                        dst = ps[:, 7, P:2 * P]
                        three(dst, (oT[:, par(1), 0, :], oT[:, par(1), 1, :]), W(l, "o"), stop=False)
                        pe.matmul(dst, two_rows[:, :], bias_rows[:, 2 * l + 1, :], start=False, stop=True).then_inc(q["y_ps"], 1)
                    if isinstance(t, int) and t == -2:
                        wait_values_split(pe, l, TILES // 2 - 1)
                    if alive(t + 2):
                        for h in range(2):
                            pe.wait_ge(q["ex"], 2 * t + (5 + h))
                            positive_wait(pe, (q["p_lo"], q["p_f"])[h], t + 2)
                            for n in range(4):
                                c = (4 * h + n) * P
                                mm = pe.transpose(ps[:, 2 + h, n * P:(n + 1) * P], probs[:, par(2), c:c + P], ident[:, :])
                            mm.then_inc(q["p_ps"], 1)

                    if isinstance(t, int) and t in TRANSPOSE:
                        transpose_group(l, TRANSPOSE.index(t))
                    if isinstance(t, int) and t in LOGITS:
                        group_logits(l, LOGITS.index(t))

                pipeline(pe, step, TILES, 6, lambda n: values(l, n))

            def transpose_group(l, g):
                q = F[l]
                if g == 0:
                    pe.wait_ge(A[l]["xt_lo"], TILES)
                elif g < 3:
                    pe.wait_ge(A[l]["sub"], 2 * TILES)
                else:
                    pe.wait_ge(q["xt_lo"], 1)
                for k in range(G):
                    pe.wait_ge(q["xh"], G * g + k + 1)
                    mm = pe.transpose(ps[:, xta_bank[g], k * P:(k + 1) * P], fx[:, g % 2, k * P:(k + 1) * P], ident[:, :])
                mm.then_inc(q["xt_ps"], 1)

            def group_logits(l, g):
                q = F[l]
                pe.wait_ge(s["small_lo"], 4)
                pe.wait_ge(q["xt_lo"], g + 1)
                if g == 1:
                    pe.wait_ge(A[l]["on"], 2 * TILES)
                if g >= 2:
                    pe.wait_ge(q["lg"], g - 1)
                for t in range(G * g, G * g + G):
                    r = slice(t * P, (t + 1) * P)
                    mm = three(ps[:, logit_bank[g % 2], t * EXPERTS:(t + 1) * EXPERTS], (xTa[:, 0, r], xTa[:, 1, r]),
                               (gate_w[:, l, 0, :], gate_w[:, l, 1, :]))
                mm.then_inc(q["lg_ps"], 1)

            def routing(l):
                q = F[l]
                transpose_group(l, GROUPS - 1)
                group_logits(l, GROUPS - 1)
                if l == 1:
                    expert1_start()
                pe.wait_ge(q["c16"], 3)
                for t in range(TILES):
                    c = (t % 8) * P
                    mm = pe.transpose(half_bank[6 + t // 8][:, c:c + P], comb16[:, t, :], ident16[:, :])
                    if t % 8 == 7:
                        mm.then_inc(q["ct_ps"], 1)

            def down(dst, h, w, first, last):
                for t in range(G):
                    r = slice(t * P, (t + 1) * P)
                    mm = three(dst[:, r], (h[:, 0, r], h[:, 1, r]), w, start=first and t == 0, stop=last, skip_group_check=True)
                return mm

            def experts0():
                q = F[0]
                pe.wait_ge(s["ch_lo"], 3)
                K = 2 * STEPS0
                LAG = 3
                with pe.Fori(0, GROUPS // 2) as i:
                    for k in range(K + LAG):
                        if k < K:
                            n = K * i + k
                            f = slice((k % STEPS0) * P, (k % STEPS0 + 1) * P)
                            tok = bass.ds(1024 * i + GT * (k // STEPS0), GT)
                            xs = (xTa[:, 0, tok], xTa[:, 1, tok])
                            if k >= 2:
                                pe.wait_ge(q["gt"], n - 1)
                            three(ps[:, k % 2, :], (wg[:, 0, f], wg[:, 1, f]), xs)
                            three(ps[:, 2 + k % 2, :], (wu[:, 0, f], wu[:, 1, f]), xs)
                            if k == 0:
                                pe.wait_ge(q["ct_a"], 1)
                                pe.wait_ge(q["ct_d"], 1)
                            pe.matmul(ps[:, 4 + k % 2, :], expert_rows[:, f], combT[:, tok], start=True, stop=True).then_inc(q["up"], 1)
                        if k >= LAG:
                            j = k - LAG
                            pe.wait_ge(q["lo"], K * i + (j + 1))
                            if j == 0:
                                pe.wait_ge(q["res"], 2 * i + 1)
                            half, f = divmod(j, STEPS0)
                            down(ps[:, 6 + half, :], hid[:, j % 4, :, :],
                                 (wd[:, 0, f * P:(f + 1) * P], wd[:, 1, f * P:(f + 1) * P]), f == 0, f == STEPS0 - 1).then_inc(q["down"], 1)

            K1 = GROUPS * STEPS1
            LAG1 = 3

            def up(e, k, n):
                q = F[1]
                g, f = divmod(k, STEPS1)
                fs = slice(f * P, (f + 1) * P)
                r = slice(g * GT, (g + 1) * GT)
                positive_wait(pe, q["act"], n - 3)
                three(ps[:, k % 4, :], (w1[:, 0, e, fs], w1[:, 1, e, fs]),
                      (xTa[:, 0, r], xTa[:, 1, r])).then_inc(q["up"], 1)

            def expert1_start():
                pe.wait_ge(s["ch_lo"], 3 + 2 * len(chunks))
                for k in range(LAG1):
                    up(0, k, k)

            def experts1():
                q = F[1]

                def output_biases(g):
                    if g >= 2:
                        pe.wait_ge(q["b2_r"], g - 1)
                    for t in range(G):
                        r = slice((G * g + t) * P, (G * g + t + 1) * P)
                        mm = pe.matmul(ps[:, 6 + g % 2, t * P:(t + 1) * P], combT[:, r], b2_rows[:, :], start=True, stop=True)
                    mm.then_inc(q["b2_ps"], 1)

                def expert(e, ahead):
                    for k in range(K1):
                        if k + LAG1 < K1:
                            up(e, k + LAG1, K1 * e + (k + LAG1))
                        elif ahead:
                            up(e + 1, k + LAG1 - K1, K1 * e + (k + LAG1))
                        if isinstance(e, int) and e == 0 and 1 <= k <= GROUPS:
                            output_biases(k - 1)
                        g, f = divmod(k, STEPS1)
                        pe.wait_ge(q["lo"], K1 * e + (k + 1))
                        if f == 0:
                            positive_wait(pe, q["res"], GROUPS * e + (g - 1))
                        down(ps[:, 4 + g % 2, :], hid[:, k % 4, :, :], (w2[:, 0, e, f, :], w2[:, 1, e, f, :]),
                             f == 0, f == STEPS1 - 1).then_inc(q["down"], 1)

                pe.wait_ge(q["ct_d"], 2)
                expert(0, True)
                with pe.Fori(1, EXPERTS - 1) as e:
                    expert(e, True)
                expert(EXPERTS - 1, False)

            make_keys(0)
            attention(0)
            routing(0)
            experts0()
            pe.wait_ge(F[0]["res"], GROUPS + 1)
            make_keys(1)
            attention(1)
            routing(1)
            experts1()


def constants():
    rows = np.zeros((P, HID0), np.float16)
    for r in (HI_ROW, LO_ROW):
        rows[r + np.arange(HID0) // M0, np.arange(HID0)] = 1
    two = np.zeros((P, P), np.float16)
    two[[0, 32]] = 1
    quad = np.arange(P)[:, None] % 32 // HD == np.arange(QUAD)[None, :]
    return {"quad_mask": quad.astype(np.float32), "ident": np.eye(P, dtype=np.float32), "expert_rows": rows, "two_rows": two,
            "iota8": np.broadcast_to(np.arange(EXPERTS, dtype=np.float32), (P, EXPERTS)).copy()}


def kernel(**inputs):
    import concourse.bacc as bacc
    from concourse.bass_utils import run_bass_kernel_spmd

    nc = bacc.Bacc("TRN2", target_bir_lowering=False, num_devices=1)
    arrays, args = {}, {}
    for name, value in {**inputs, **constants()}.items():
        v = np.ascontiguousarray(value)
        arrays[f"in_{name}"] = v
        args[name] = nc.dram_tensor(f"in_{name}", v.shape, mybir.dt.from_np(v.dtype), kind="ExternalInput").ap()
    out = nc.dram_tensor("out", inputs["x"].shape, F32, kind="ExternalOutput").ap()
    build(nc, args, out)
    r = run_bass_kernel_spmd(nc, [arrays], core_ids=[0])
    return r.results[0]["out"]
```
